# Optimizing a Trainium2 kernel written in Bass

```python
import numpy as np
import jax
import jax.numpy as jnp

def _softmax(x, axis=-1):
    return jax.nn.softmax(x, axis=axis)

def _gelu(x):
    return jax.nn.gelu(x, approximate=True)

def _silu(x):
    return jax.nn.silu(x)

def _sigmoid(x):
    return jax.nn.sigmoid(x)

def _layernorm(x, axis=-1, eps=1e-05):
    m = jnp.mean(x, axis=axis, keepdims=True)
    v = jnp.var(x, axis=axis, keepdims=True)
    return (x - m) / jnp.sqrt(v + eps)

def _scatter_add(tgt, idx, src, axis=0):
    return tgt.at[idx].add(src)

def _segment_sum(src, seg, n):
    return jax.ops.segment_sum(src, seg, n)
kernel_name = 'mk_macaron_d1_jaxref_r4_7a335f'

def setup_inputs(seed: int=0):
    np.random.seed(seed)
    _w = jnp.asarray

    def _L0_attn_setup():
        import jax, jax.numpy as jnp
        import numpy as np
        _DENSE_LOCAL_W = 32
        _DYADIC = [48, 64, 96, 128, 192, 64, 96, 128, 192, 256, 384]
        OFFSETS = sorted(set(range(_DENSE_LOCAL_W + 1)) | set(_DYADIC))
        B, N, D, H = (2, 1024, 256, 16)
        HD = D // H
        NEG = -1e+30

        def _shift(t, o):
            if o == 0:
                return t
            n = t.shape[2]
            return jnp.pad(t, ((0, 0), (0, 0), (o, 0), (0, 0)))[:, :, :n]
        key = jax.random.key(seed)
        ks = jax.random.split(key, 9)
        alphas = jnp.linspace(0.2, 2.0, H)
        delta = jnp.log1p(jnp.asarray(OFFSETS, dtype=jnp.float32))
        pos_bias = -delta[:, None] * alphas[None, :]
        return {'x': jax.random.normal(ks[0], (B, N, D), jnp.float32), 'qkv_w': jax.random.normal(ks[1], (3 * D, D), jnp.float32) * 0.02, 'qkv_b': jax.random.normal(ks[2], (3 * D,), jnp.float32) * 0.01, 'out_w': jax.random.normal(ks[3], (D, D), jnp.float32) * 0.02, 'out_b': jnp.zeros((D,), jnp.float32), 'gate_w': jax.random.normal(ks[4], (D, D), jnp.float32) * 0.02, 'gate_b': jnp.zeros((D,), jnp.float32), 'pos_bias': pos_bias, 'scale_embed': jax.random.normal(ks[5], (len(OFFSETS), HD), jnp.float32) * 0.02, 'if_gain': 1.0 + jax.random.normal(ks[6], (H,), jnp.float32) * 0.05}
    _L0_attn_in = _L0_attn_setup()

    def _L0_ffn_setup():
        import jax, jax.numpy as jnp
        import numpy as np
        DIM = 256

        def _reference_tuple_inner(x, W_r, W_k, W_v, mu_r, mu_k):
            B, T, C = x.shape
            x_prev = jnp.concatenate([jnp.zeros((B, 1, C), x.dtype), x[:, :-1, :]], axis=1)
            xr = mu_r * x + (1.0 - mu_r) * x_prev
            xk = mu_k * x + (1.0 - mu_k) * x_prev
            r = jax.nn.sigmoid(jnp.einsum('btc,dc->btd', xr, W_r))
            k = jnp.einsum('btc,dc->btd', xk, W_k)
            k_act = jnp.square(jax.nn.relu(k))
            out = r * jnp.einsum('btc,dc->btd', k_act, W_v)
            new_state = x[:, -1, :]
            return (out, new_state)
        key = jax.random.key(seed)
        ks = jax.random.split(key, 6)
        B, T, C = (8, 512, DIM)
        x = jax.random.normal(ks[0], (B, T, C), dtype=jnp.float32)
        s = 1.0 / np.sqrt(C)
        W_r = jax.random.uniform(ks[1], (C, C), jnp.float32, -s, s)
        W_k = jax.random.uniform(ks[2], (C, C), jnp.float32, -s, s)
        W_v = jax.random.uniform(ks[3], (C, C), jnp.float32, -s, s)
        mu_r = jax.random.uniform(ks[4], (C,), jnp.float32)
        mu_k = jax.random.uniform(ks[5], (C,), jnp.float32)
        return {'x': x, 'W_r': W_r, 'W_k': W_k, 'W_v': W_v, 'mu_r': mu_r, 'mu_k': mu_k}
    _L0_ffn_in = _L0_ffn_setup()
    _d = {'L0_attn_x': _L0_attn_in['x'], 'L0_attn_qkv_w': _L0_attn_in['qkv_w'], 'L0_attn_qkv_b': _L0_attn_in['qkv_b'], 'L0_attn_out_w': _L0_attn_in['out_w'], 'L0_attn_out_b': _L0_attn_in['out_b'], 'L0_attn_gate_w': _L0_attn_in['gate_w'], 'L0_attn_gate_b': _L0_attn_in['gate_b'], 'L0_attn_pos_bias': _L0_attn_in['pos_bias'], 'L0_attn_scale_embed': _L0_attn_in['scale_embed'], 'L0_attn_if_gain': _L0_attn_in['if_gain'], 'L0_ffn_W_r': _L0_ffn_in['W_r'], 'L0_ffn_W_k': _L0_ffn_in['W_k'], 'L0_ffn_W_v': _L0_ffn_in['W_v'], 'L0_ffn_mu_r': _L0_ffn_in['mu_r'], 'L0_ffn_mu_k': _L0_ffn_in['mu_k']}
    _x0 = _d['L0_attn_x']
    _d['L0_attn_x'] = jax.random.normal(jax.random.fold_in(jax.random.key(seed), 1), (8, 1024, 256), dtype=_x0.dtype)
    del _x0
    return _d

def reference(L0_attn_x, L0_attn_qkv_w, L0_attn_qkv_b, L0_attn_out_w, L0_attn_out_b, L0_attn_gate_w, L0_attn_gate_b, L0_attn_pos_bias, L0_attn_scale_embed, L0_attn_if_gain, L0_ffn_W_r, L0_ffn_W_k, L0_ffn_W_v, L0_ffn_mu_r, L0_ffn_mu_k):

    def _L0_attn_ref(x, qkv_w, qkv_b, out_w, out_b, gate_w, gate_b, pos_bias, scale_embed, if_gain):
        import jax, jax.numpy as jnp
        import numpy as np
        _DENSE_LOCAL_W = 32
        _DYADIC = [48, 64, 96, 128, 192, 64, 96, 128, 192, 256, 384]
        OFFSETS = sorted(set(range(_DENSE_LOCAL_W + 1)) | set(_DYADIC))
        B, N, D, H = (2, 1024, 256, 16)
        HD = D // H
        NEG = -1e+30

        def _shift(t, o):
            if o == 0:
                return t
            n = t.shape[2]
            return jnp.pad(t, ((0, 0), (0, 0), (o, 0), (0, 0)))[:, :, :n]
        b, n, d = x.shape
        qkv = x @ qkv_w.T + qkv_b
        q, k, v = jnp.split(qkv, 3, axis=-1)
        heads = lambda t: t.reshape(b, n, H, HD).transpose(0, 2, 1, 3)
        q, k, v = (heads(q), heads(k), heads(v))
        inv = 1.0 / jnp.sqrt(jnp.asarray(HD, x.dtype))
        qs = jnp.einsum('bhnd,od->bhno', q, scale_embed)
        pos = jnp.arange(n)
        logits = []
        for i, o in enumerate(OFFSETS):
            qk = jnp.einsum('bhnd,bhnd->bhn', q, _shift(k, o))
            lg = qk * inv * (1.0 + qs[..., i]) + pos_bias[i][None, :, None]
            lg = jnp.where(pos[None, None, :] >= o, lg, NEG)
            logits.append(lg)
        logits = jnp.stack(logits, axis=-1)
        p = jax.nn.softmax(logits, axis=-1)
        out = jnp.zeros_like(q)
        for i, o in enumerate(OFFSETS):
            out = out + p[..., i][..., None] * _shift(v, o)
        out = out * if_gain[None, :, None, None]
        out_flat = out.transpose(0, 2, 1, 3).reshape(b, n, d)
        gate = jax.nn.sigmoid(x @ gate_w.T + gate_b)
        return out_flat * gate @ out_w.T + out_b

    def _L0_ffn_ref(x, W_r, W_k, W_v, mu_r, mu_k):
        import jax, jax.numpy as jnp
        import numpy as np
        DIM = 256

        def _reference_tuple_inner(x, W_r, W_k, W_v, mu_r, mu_k):
            B, T, C = x.shape
            x_prev = jnp.concatenate([jnp.zeros((B, 1, C), x.dtype), x[:, :-1, :]], axis=1)
            xr = mu_r * x + (1.0 - mu_r) * x_prev
            xk = mu_k * x + (1.0 - mu_k) * x_prev
            r = jax.nn.sigmoid(jnp.einsum('btc,dc->btd', xr, W_r))
            k = jnp.einsum('btc,dc->btd', xk, W_k)
            k_act = jnp.square(jax.nn.relu(k))
            out = r * jnp.einsum('btc,dc->btd', k_act, W_v)
            new_state = x[:, -1, :]
            return (out, new_state)
        return _reference_tuple_inner(x, W_r, W_k, W_v, mu_r, mu_k)[0]
    x = L0_attn_x
    x = x + 0.5 * _L0_ffn_ref(_layernorm(x, axis=-1), L0_ffn_W_r, L0_ffn_W_k, L0_ffn_W_v, L0_ffn_mu_r, L0_ffn_mu_k)
    x = x + _L0_attn_ref(_layernorm(x, axis=-1), L0_attn_qkv_w, L0_attn_qkv_b, L0_attn_out_w, L0_attn_out_b, L0_attn_gate_w, L0_attn_gate_b, L0_attn_pos_bias, L0_attn_scale_embed, L0_attn_if_gain)
    x = x + 0.5 * _L0_ffn_ref(_layernorm(x, axis=-1), L0_ffn_W_r, L0_ffn_W_k, L0_ffn_W_v, L0_ffn_mu_r, L0_ffn_mu_k)
    return x

_drawn_inputs = setup_inputs


def setup_inputs(seed=0):
    import zlib

    import numpy as np

    out = dict(_drawn_inputs(seed))
    spreads = {'L0_attn_out_b': (0.0, 0.1), 'L0_attn_gate_b': (0.0, 0.8)}
    factors = {'L0_attn_qkv_w': 2.684,
     'L0_attn_qkv_b': 8.0,
     'L0_attn_gate_w': 8.0,
     'L0_attn_pos_bias': 2.86,
     'L0_attn_scale_embed': 8.0,
     'L0_attn_if_gain': 8.0,
     'L0_ffn_W_r': 3.186,
     'L0_ffn_mu_r': 6.422}
    for name, (base, spread) in spreads.items():
        noise = np.random.default_rng([zlib.crc32(name.encode()), seed]).standard_normal(out[name].shape)
        drawn = base * np.exp(spread * noise) if base else spread * noise
        out[name] = jnp.asarray(drawn.astype(out[name].dtype))
    for name, factor in factors.items():
        out[name] = (out[name] * factor).astype(out[name].dtype)
    return out
```

```python
import concourse.bass as bass
from concourse import mybir
from contextlib import ExitStack

F32 = mybir.dt.float32
ALU = mybir.AluOpType
ACT = mybir.ActivationFunctionType
AX = mybir.AxisListType

P = 128
B, N, D, H = 8, 1024, 256, 16
HD = D // H
DC = D // P
HC = H // DC
NT = N // P
TILES = B * NT
EPS = 1e-5

NEAR = 33
SUB = 32
WIN = 2 * SUB
NSUB = P // SUB
FAR = [48, 64, 96, 128, 192, 256, 384]
NO = NEAR + len(FAR)
NF = len(FAR)
LOC = NEAR * H
ALL = NO * H
BIAS_TILES = FAR[-1] // P + 1
GROUP = 4
NG = TILES // GROUP
LAG_S, LAG_W, LAG_V = 1, 2, 3


def wait(eng, sem, value):
    if isinstance(value, int) and value <= 0:
        return
    eng.wait_ge(sem, value)


def waits(eng, passed, *pairs):
    for sem, value in pairs:
        if isinstance(value, int) and value <= 0:
            continue
        eng.wait_ge(sem, value).then_inc(passed, 1)


def ffn_phase(nc, X, x_in, out, w_r, w_k, w_v, mu_r, mu_k, ident_in, tag, stats_after):
    ctx = ExitStack()
    with ctx:
        def sb(name, shape):
            return ctx.enter_context(nc.sbuf_tensor(tag + name, shape, F32))

        def pb(name, shape):
            return ctx.enter_context(nc.psum_tensor(tag + name, shape, F32))

        def sem(name):
            return ctx.enter_context(nc.semaphore(tag + name))

        GT = GROUP * P
        wr = sb("wr", [P, DC, D])
        wk = sb("wk", [P, DC, D])
        wv = sb("wv", [P, DC, D])
        mur = sb("mur", [P, DC])
        muk = sb("muk", [P, DC])
        ident = sb("ident", [P, P])
        mhalf = sb("mhalf", [P, GROUP])
        st = sb("st", [P, 2, GROUP, 6])
        mv = sb("mv", [P, 2, GROUP, 2])
        ve = sb("ve", [P, 2, GROUP])
        rstd = sb("rstd", [P, 2, GROUP])
        xn = sb("xn", [P, 2, GROUP, D])
        xT = sb("xT", [P, 2, DC, 1 + GT])
        dx = sb("dx", [P, 2, DC, GT])
        xr = sb("xr", [P, 2, DC, GT])
        xk = sb("xk", [P, 2, DC, GT])
        kr = sb("kr", [P, DC, GT])
        ka = sb("ka", [P, 2, DC, GT])
        th = sb("th", [P, 2, GROUP, D])
        rv = sb("rv", [P, 2, GROUP, D])
        st2 = sb("st2", [P, 2, GROUP, 6])
        mv2 = sb("mv2", [P, 2, GROUP, 2])
        ve2 = sb("ve2", [P, 2, GROUP])

        psT = pb("psT", [P, DC, GT])
        psK = pb("psK", [P, DC, GT])
        psR = pb("psR", [P, GROUP, D])
        psV = pb("psV", [P, GROUP, D])

        s_w = sem("weights_loaded")
        s_x = sem("x_loaded")
        s_c = sem("constants_set")
        s_st = sem("stats_of_tile")
        s_mv = sem("mean_var_of_tile")
        s_ve = sem("var_plus_eps")
        s_rs = sem("rstd_ready")
        s_xn = sem("xn_ready")
        s_T = sem("transposed_in_psum")
        s_xT = sem("xT_ready")
        s_dx = sem("dx_ready")
        s_mix = sem("mixed_ready")
        s_K = sem("k_in_psum")
        s_kr = sem("relu_done")
        s_ka = sem("squared_ready")
        s_R = sem("r_in_psum")
        s_th = sem("tanh_ready")
        s_V = sem("v_in_psum")
        s_rv = sem("rv_done")
        s_res = sem("residual_done")
        s_st2 = sem("new_stats")
        s_mv2 = sem("new_mean_var")
        s_ve2 = sem("new_var_plus_eps")
        s_rs2 = sem("new_rstd")
        s_out = sem("stored")
        s_passed = sem("waits_passed")

        block = ctx.enter_context(nc.Block())
        GB = NT // GROUP

        @block.sync
        def _(sp):
            sp.dma_start(wk[:, :, :], w_k.rearrange("(c p) n -> p c n", p=P)).then_inc(s_w, 16)
            sp.dma_start(wr[:, :, :], w_r.rearrange("(c p) n -> p c n", p=P)).then_inc(s_w, 16)
            sp.dma_start(wv[:, :, :], w_v.rearrange("(c p) n -> p c n", p=P)).then_inc(s_w, 16)
            sp.dma_start(ident[:, :], ident_in).then_inc(s_w, 16)
            sp.dma_start(mur[:, :], mu_r).then_inc(s_w, 16)
            sp.dma_start(muk[:, :], mu_k).then_inc(s_w, 16)
            if x_in is not None:
                xv = x_in.rearrange("(t p) d -> p t d", p=P)
                for g in range(NG):
                    wait(sp, s_x, 16 * g)
                    sp.dma_start(X[:, g * GROUP:(g + 1) * GROUP, :],
                                 xv[:, g * GROUP:(g + 1) * GROUP, :]).then_inc(s_x, 16)
            if out is not None:
                ov = out.rearrange("(t p) d -> p t d", p=P)
                for g in range(NG):
                    sp.wait_ge(s_res, GROUP * (g + 1))
                    sp.dma_start(ov[:, g * GROUP:(g + 1) * GROUP, :],
                                 X[:, g * GROUP:(g + 1) * GROUP, :]).then_inc(s_out, 16)
                sp.wait_ge(s_out, 16 * NG)
            sp.wait_ge(s_w, 96)

        @block.vector
        def _(dve):
            nc.vector.memset(mhalf[:, :], -0.5).then_inc(s_c, 1)
            nc.vector.memset(xT[:, 0, :, 0:1], 0.0).then_inc(s_c, 1)

            def norm(G, par):
                if x_in is not None:
                    waits(dve, s_passed, (s_x, 16 * (G + 1)))
                for u in range(GROUP):
                    nc.vector.bn_stats(st[:, par, u, :], X[:, G * GROUP + u, :]).then_inc(s_st, 1)
                for u in range(GROUP):
                    waits(dve, s_passed, (s_st, GROUP * G + u + 1))
                    nc.vector.bn_aggr(mv[:, par, u, :], st[:, par, u, :]).then_inc(s_mv, 1)
                dve.wait_ge(s_mv, GROUP * (G + 1))
                nc.vector.tensor_scalar(ve[:, par, :], mv[:, par, :, 1], EPS, None, ALU.add).then_inc(s_ve, 1)
                dve.wait_ge(s_rs, G + 1)
                wait(dve, s_T, G - 1)
                for u in range(GROUP):
                    last = nc.vector.tensor_scalar(xn[:, par, u, :], X[:, G * GROUP + u, :],
                                                   mv[:, par, u, 0:1], rstd[:, par, u:u + 1],
                                                   ALU.subtract, ALU.mult)
                last.then_inc(s_xn, 1)

            def mix(G, par):
                dve.wait_ge(s_dx, G + 1)
                wait(dve, s_V, G - 1)
                for dst, mu in ((xk, muk), (xr, mur)):
                    for c in range(DC):
                        nc.vector.scalar_tensor_tensor(dst[:, par, c, :], dx[:, par, c, :], mu[:, c:c + 1],
                                                       xT[:, par, c, 0:GT], ALU.mult, ALU.add).then_inc(s_mix, 1)

            def final(G, par):
                dve.wait_ge(s_th, G + 1)
                dve.wait_ge(s_V, G + 1)
                for u in range(GROUP):
                    nc.vector.scalar_tensor_tensor(rv[:, par, u, :], th[:, par, u, :], 1.0, psV[:, u, :],
                                                   ALU.add, ALU.mult).then_inc(s_rv, 1)
                for u in range(GROUP):
                    dve.wait_ge(s_rv, GROUP * G + u + 1)
                    x = X[:, G * GROUP + u, :]
                    nc.vector.scalar_tensor_tensor(x, rv[:, par, u, :], 0.25, x,
                                                   ALU.mult, ALU.add).then_inc(s_res, 1)
                if stats_after is None:
                    return
                for u in range(GROUP):
                    waits(dve, s_passed, (s_res, GROUP * G + u + 1))
                    nc.vector.bn_stats(st2[:, par, u, :], X[:, G * GROUP + u, :]).then_inc(s_st2, 1)
                waits(dve, s_passed, (s_rs2, 2 * (G - 1)))
                for u in range(GROUP):
                    waits(dve, s_passed, (s_st2, GROUP * G + u + 1))
                    nc.vector.bn_aggr(mv2[:, par, u, :], st2[:, par, u, :]).then_inc(s_mv2, 1)
                dve.wait_ge(s_mv2, GROUP * (G + 1))
                nc.vector.tensor_scalar(ve2[:, par, :], mv2[:, par, :, 1], EPS, None, ALU.add).then_inc(s_ve2, 1)

            dve.wait_ge(s_w, 96)
            dve.wait_ge(s_c, 2)
            norm(0, 0)
            norm(1, 1)
            mix(0, 0)

            def ahead(G, g):
                norm(G + 2, g)
                mix(G + 1, 1 - g)
                final(G, g)

            for g in range(GB):
                ahead(g, g)
            with dve.Fori(1, B - 1) as b:
                for g in range(GB):
                    ahead(b * GB + g, g)
            mix(NG - 1, 1)
            final(NG - 2, 0)
            final(NG - 1, 1)

        @block.gpsimd
        def _(pool):
            pool.wait_ge(s_c, 2)

            def rs(G, par):
                pool.wait_ge(s_ve, G + 1)
                wait(pool, s_xn, G - 1)
                nc.gpsimd.tensor_tensor(rstd[:, par, :], ve[:, par, :], mhalf[:, :], ALU.pow).then_inc(s_rs, 1)

            def diff(G, par):
                pool.wait_ge(s_xT, G + 1)
                wait(pool, s_mix, 2 * DC * (G - 1))
                nc.gpsimd.tensor_tensor(dx[:, par, :, :], xT[:, par, :, 1:1 + GT], xT[:, par, :, 0:GT],
                                        ALU.subtract).then_inc(s_dx, 1)

            def new(G, par):
                if stats_after is None:
                    return
                mean_all, rstd_all = stats_after
                pool.wait_ge(s_ve2, G + 1)
                nc.gpsimd.tensor_copy(mean_all[:, bass.ds(G * GROUP, GROUP)], mv2[:, par, :, 0]).then_inc(s_rs2, 1)
                nc.gpsimd.tensor_tensor(rstd_all[:, bass.ds(G * GROUP, GROUP)], ve2[:, par, :], mhalf[:, :],
                                        ALU.pow).then_inc(s_rs2, 1)

            rs(0, 0)
            rs(1, 1)
            diff(0, 0)
            def ahead(G, g):
                rs(G + 2, g)
                diff(G + 1, 1 - g)
                new(G, g)

            for g in range(GB):
                ahead(g, g)
            with pool.Fori(1, B - 1) as b:
                for g in range(GB):
                    ahead(b * GB + g, g)
            diff(NG - 1, 1)
            new(NG - 2, 0)
            new(NG - 1, 1)

        @block.scalar
        def _(act):
            def xt(G, par):
                act.wait_ge(s_T, G + 1)
                wait(act, s_mix, 2 * DC * (G - 1))
                last = nc.scalar.activation(xT[:, par, :, 1:1 + GT], psT[:, :, :], ACT.Copy)
                if par:
                    act.wait_ge(s_xT, G)
                    last = nc.scalar.activation(xT[:, 1, :, 0:1], xT[:, 0, :, GT:GT + 1], ACT.Copy)
                last.then_inc(s_xT, 1)

            def rest(G, par):
                act.wait_ge(s_K, G + 1)
                wait(act, s_ka, G)
                nc.scalar.activation(kr[:, :, :], psK[:, :, :], ACT.Relu).then_inc(s_kr, 1)
                act.wait_ge(s_kr, G + 1)
                wait(act, s_V, G - 1)
                nc.scalar.activation(ka[:, par, :, :], kr[:, :, :], ACT.Square).then_inc(s_ka, 1)
                act.wait_ge(s_R, G + 1)
                wait(act, s_rv, GROUP * (G - 1))
                nc.scalar.activation(th[:, par, :, :], psR[:, :, :], ACT.Tanh, scale=0.5).then_inc(s_th, 1)

            xt(0, 0)
            def ahead(G, g):
                xt(G + 1, 1 - g)
                rest(G, g)

            for g in range(GB):
                ahead(g, g)
            with act.Fori(1, B - 1) as b:
                for g in range(GB):
                    ahead(b * GB + g, g)
            xt(NG - 1, 1)
            rest(NG - 2, 0)
            rest(NG - 1, 1)

        @block.tensor
        def _(pe):
            def tr(G, par):
                pe.wait_ge(s_xn, G + 1)
                wait(pe, s_xT, G)
                for c in range(DC):
                    for u in range(GROUP):
                        last = nc.tensor.transpose(psT[:, c, u * P:(u + 1) * P], xn[:, par, u, c * P:(c + 1) * P],
                                                   ident[:, :])
                last.then_inc(s_T, 1)

            def products(G, par):
                pe.wait_ge(s_mix, 2 * DC * G + DC)
                wait(pe, s_kr, G)
                for e in range(DC):
                    for c in range(DC):
                        last = nc.tensor.matmul(psK[:, e, :], wk[:, c, e * P:(e + 1) * P], xk[:, par, c, :],
                                                start=(c == 0), stop=(c == DC - 1))
                last.then_inc(s_K, 1)
                pe.wait_ge(s_mix, 2 * DC * (G + 1))
                wait(pe, s_th, G)
                for u in range(GROUP):
                    for c in range(DC):
                        last = nc.tensor.matmul(psR[:, u, :], xr[:, par, c, u * P:(u + 1) * P], wr[:, c, :],
                                                start=(c == 0), stop=(c == DC - 1))
                last.then_inc(s_R, 1)
                pe.wait_ge(s_ka, G + 1)
                wait(pe, s_rv, GROUP * G)
                for u in range(GROUP):
                    for c in range(DC):
                        last = nc.tensor.matmul(psV[:, u, :], ka[:, par, c, u * P:(u + 1) * P], wv[:, c, :],
                                                start=(c == 0), stop=(c == DC - 1))
                last.then_inc(s_V, 1)

            pe.wait_ge(s_w, 96)
            tr(0, 0)
            def ahead(G, g):
                tr(G + 1, 1 - g)
                products(G, g)

            for g in range(GB):
                ahead(g, g)
            with pe.Fori(1, B - 1) as b:
                for g in range(GB):
                    ahead(b * GB + g, g)
            tr(NG - 1, 1)
            products(NG - 2, 0)
            products(NG - 1, 1)


def attention_phase(nc, X, mean_all, rstd_all, w_qkv, w_gate, w_out, qk_bias, v_bias, gate_bias, out_bias,
                    gain, scale_rows, pos_rows, masks, ident_in, head_mask, quad_mask, s_dram, p_dram):
    ctx = ExitStack()
    with ctx:
        def sb(name, shape):
            return ctx.enter_context(nc.sbuf_tensor("a_" + name, shape, F32))

        def pb(name, shape):
            return ctx.enter_context(nc.psum_tensor("a_" + name, shape, F32))

        def sem(name):
            return ctx.enter_context(nc.semaphore("a_" + name))

        KEYS = SUB + P
        wqkv = sb("wqkv", [P, DC, 3 * D])
        wg = sb("wg", [P, DC, D])
        wo = sb("wo", [P, DC, D])
        bqk = sb("bqk", [P, 2 * DC])
        bv = sb("bv", [P, D])
        bg = sb("bg", [P, DC])
        ob = sb("ob", [P, D])
        gn = sb("gn", [P, DC])
        se = sb("se", [P, NO * HC])
        ident = sb("ident", [P, P])
        hm = sb("hm", [P, HC])
        qm = sb("qm", [P, 4, HD])
        bias = sb("bias", [P, BIAS_TILES, ALL])
        xn = sb("xn", [P, D])
        xT = sb("xT", [P, DC, P])
        qT = sb("qT", [P, DC, P])
        kT = sb("kT", [P, DC, P])
        kbd = sb("kbd", [P, 2, DC, P, HC])
        gate = sb("gate", [P, 4, DC, P])
        qtok = sb("qtok", [P, 2, D])
        KV = sb("KV", [P, NT, 2 * D])
        S64 = sb("S64", [P, 4, 2 * D])
        S48 = sb("S48", [P, 2, 2 * D])
        S96 = sb("S96", [P, 2, 2 * D])
        vp = sb("vp", [P, 2, H // 2, 2, 2 * HD])
        vrep = sb("vrep", [P, D])
        vh = sb("vh", [P, 2, H // 4, 4, HD])
        ssb = sb("ssb", [P, WIN, H])
        qs1 = sb("qs1", [P, 2, NO, H])
        lg = sb("lg", [P, NO, H])
        ex = sb("ex", [P, 2, NO, H])
        mx = sb("mx", [P, 2, H])
        sm = sb("sm", [P, 2, H])
        rs = sb("rs", [P, 2, H])
        fqk = sb("fqk", [P, NF, D])
        fpv = sb("fpv", [P, NF, D])
        ftok = sb("ftok", [P, 2, D])
        pd = sb("pd", [P, KEYS, H])
        ph = sb("ph", [SUB, H, SUB])
        pT = sb("pT", [P, 2, 4, P])
        phT = sb("phT", [P, 4, SUB])
        at = sb("at", [P, DC, P])
        res = sb("res", [P, D])

        psX = pb("psX", [P, 4, P])
        psP = pb("psP", [P, 4, P])
        psG = pb("psG", [P, 4, P])
        psS = pb("psS", [P, DC, 512])
        psT = pb("psT", [P, 2, 4, P])
        psO = pb("psO", [P, 4, P])

        names = """weights scaled biases ones zeros xn xT_ps xT qk_ps qT kT gv_ps v_ready gate tok_ps qtok ktok
            shift48 shift64 shift96 vrep vp vh kbd0 kbd1 qs_ps qs1 s_ps ssb s_stored0 s_stored1 near0 near1
            fqk far_lg prod biased mx shifted ex sm rs p_ready fpv ftok p_stored0 p_stored1 band0 band1
            pt_ps pt_halo_ps ph pv_used pT phT o_ps at out_ps res x_new passed sp_passed""".split()
        S = {n: sem(n) for n in names}
        block = ctx.enter_context(nc.Block())

        def rows(eng, step, ends=()):
            for t in range(NT):
                step(t, t, True)
            with eng.Fori(1, B) as b:
                for t in range(NT):
                    step(b * NT + t, t, True)
            for t in range(LAG_V):
                step(TILES + t, t, False)

        def there(T):
            return not (isinstance(T, int) and T < 0)

        def has_s(T):
            return not isinstance(T, int) or 0 <= T - LAG_S < TILES

        def has_w(T):
            return not isinstance(T, int) or 0 <= T - LAG_W < TILES

        def has_v(T):
            return not isinstance(T, int) or 0 <= T - LAG_V < TILES

        def dma_count(T, t, per=1):
            return 16 * per * ((T - t) // 2 + t // 2 + 1) if isinstance(T, int) else \
                (T - t) * (8 * per) + 16 * per * (t // 2 + 1)

        @block.sync
        def _(sp):
            loads = [(wqkv[:, :, :], w_qkv.rearrange("(c p) n -> p c n", p=P)),
                     (wg[:, :, :], w_gate.rearrange("(c p) n -> p c n", p=P)),
                     (wo[:, :, :], w_out.rearrange("(c p) n -> p c n", p=P)),
                     (bqk[:, :], qk_bias), (bg[:, :], gate_bias), (gn[:, :], gain),
                     (bv[:, :], v_bias.partition_broadcast(P)), (ob[:, :], out_bias.partition_broadcast(P)),
                     (se[:, :], scale_rows), (ident[:, :], ident_in), (hm[:, :], head_mask),
                     (qm[:, :, :], quad_mask), (ssb[:, 0:NO, :], pos_rows.partition_broadcast(P)),
                     (ex[:, 0, :, 0:BIAS_TILES], masks)]
            for dst, src in loads:
                sp.dma_start(dst, src).then_inc(S["weights"], 16)
            sp.wait_ge(S["zeros"], 1)
            for par in range(2):
                sp.dma_start(p_dram[par].rearrange("(p k) -> p k", p=P),
                             pd[:, 0:WIN, :].rearrange("p k h -> p (k h)")).then_inc(S[f"p_stored{par}"], 16)

            ROW = WIN * H
            def band(dram):
                return bass.AP(dram.tensor, dram.offset, [[SUB * ROW, NSUB], [ROW + H, SUB], [1, LOC]])

            def step(T, t, first):
                par = t % 2
                if first:
                    waits(sp, S["sp_passed"], (S["ktok"], T + 1),
                          (S["v_ready"], T + 1))
                    prev, cur = (t - 1) % NT, t
                    for sh, buf, slots, name in ((48, S48, 2, "shift48"), (64, S64, 4, "shift64"),
                                                 (96, S96, 2, "shift96")):
                        waits(sp, S["sp_passed"], (S["fpv"], T + 1 - (slots if slots == 2 else slots - 1)))
                        sp.dma_start(buf[0:sh, t % slots, :], KV[P - sh:P, prev, :]).then_inc(S[name], 16)
                        sp.dma_start(buf[sh:P, t % slots, :], KV[0:P - sh, cur, :]).then_inc(S[name], 16)
                if has_w(T):
                    w, wt = T - LAG_W, (t - LAG_W) % NT
                    waits(sp, S["sp_passed"], (S["vh"], w))
                    for j in range(4):
                        sp.dma_start(vrep[SUB * j:SUB * (j + 1), :],
                                     KV[P - SUB:P, (wt - 1) % NT, D:2 * D]).then_inc(S["vrep"], 16)
                    waits(sp, S["sp_passed"], (S["pt_halo_ps"], w),
                          (S[f"p_stored{wt % 2}"], dma_count(w, wt) + 16))
                    for s in range(NSUB):
                        sp.dma_start(pd[SUB * s:SUB * (s + 1), SUB * s:SUB * s + WIN, :]
                                     .rearrange("p k h -> p (k h)"),
                                     p_dram[wt % 2].rearrange("(p k) -> p k", p=P)[SUB * s:SUB * (s + 1), :])\
                            .then_inc(S[f"band{wt % 2}"], 16)
                if has_s(T):
                    m, mt = T - LAG_S, (t - LAG_S) % NT
                    mp = mt % 2
                    waits(sp, S["sp_passed"], (S["p_ready"], m + 1),
                          (S[f"band{mp}"], dma_count(m, mt, NSUB) - 16 * NSUB),
                          (S[f"p_stored{mp}"], dma_count(m, mt)))
                    sp.dma_start(band(p_dram[mp]), ex[:, mp, 0:NEAR, :].rearrange("p k h -> p (k h)"))\
                        .then_inc(S[f"p_stored{mp}"], 16)
                if first:
                    waits(sp, S["sp_passed"], (S["ssb"], T + 1),
                          (S[f"near{par}"], dma_count(T, t) - 16))
                    sp.dma_start(s_dram[par].rearrange("(p k) -> p k", p=P),
                                 ssb[:, :, :].rearrange("p k h -> p (k h)")).then_inc(S[f"s_stored{par}"], 16)
                    waits(sp, S["sp_passed"], (S[f"s_stored{par}"], dma_count(T, t)),
                          (S["shifted"], T))
                    sp.dma_start(lg[:, 0:NEAR, :].rearrange("p k h -> p (k h)"),
                                 band(s_dram[par])).then_inc(S[f"near{par}"], 16)

            rows(sp, step)

        @block.vector
        def _(dve):
            dve.wait_ge(S["weights"], 16 * 14)
            for c in range(DC):
                nc.vector.tensor_scalar(wo[:, c, :], wo[:, c, :], gn[:, c:c + 1], 0.5, ALU.mult, ALU.mult)\
                    .then_inc(S["scaled"], 1)
            nc.vector.tensor_scalar(bg[:, :], bg[:, :], 0.5, None, ALU.mult).then_inc(S["scaled"], 1)
            nc.vector.tensor_copy(bias[:, BIAS_TILES - 1, :], ssb[:, 0:NO, :].rearrange("p o h -> p (o h)"))\
                .then_inc(S["biases"], 1)
            for v in range(BIAS_TILES - 1):
                nc.vector.tensor_tensor(bias[:, v, :].rearrange("p (o h) -> p o h", h=H), ssb[:, 0:NO, :],
                                        ex[:, 0, :, v:v + 1].to_broadcast([P, NO, H]), ALU.add)\
                    .then_inc(S["biases"], 1)
            dve.wait_ge(S["biases"], BIAS_TILES)
            dve.wait_ge(S["zeros"], 2)

            def step(T, t, first):
                par = t % 2
                m, mt = T - LAG_S, (t - LAG_S) % NT
                mp = mt % 2
                j, jt = T - LAG_V, (t - LAG_V) % NT
                if first:
                    wait(dve, S["xT_ps"], T)
                    nc.vector.tensor_scalar(xn[:, :], X[:, T, :], mean_all[:, bass.ds(T, 1)],
                                            rstd_all[:, bass.ds(T, 1)], ALU.subtract, ALU.mult)\
                        .then_inc(S["xn"], 1)
                if has_s(T - 1):
                    f, ft = m - 1, (mt - 1) % NT
                    dve.wait_ge(S["fpv"], f + 1)
                    wait(dve, S["o_ps"], f - 1)
                    nc.vector.tensor_reduce(ftok[:, ft % 2, :], fpv[:, :, :].rearrange("p o d -> p d o"),
                                            AX.X, ALU.add).then_inc(S["ftok"], 1)
                if first:
                    dve.wait_ge(S["qk_ps"], T + 1)
                    wait(dve, S["s_ps"], T)
                    nc.vector.tensor_tensor(qT[:, :, :], psP[:, 0:DC, :],
                                            bqk[:, 0:DC].unsqueeze(2).to_broadcast([P, DC, P]), ALU.add)\
                        .then_inc(S["qT"], 1)
                    nc.vector.tensor_tensor(kT[:, :, :], psP[:, DC:2 * DC, :],
                                            bqk[:, DC:2 * DC].unsqueeze(2).to_broadcast([P, DC, P]), ALU.add)\
                        .then_inc(S["kT"], 1)
                if has_v(T):
                    dve.wait_ge(S["o_ps"], j + 1)
                    wait(dve, S["out_ps"], j)
                    nc.vector.scalar_tensor_tensor(at[:, :, :], gate[:, jt % 4, :, :], 1.0, psO[:, 0:DC, :],
                                                   ALU.add, ALU.mult).then_inc(S["at"], 1)
                if first:
                    dve.wait_ge(S["gv_ps"], T + 1)
                    wait(dve, S["fpv"], T + 1 - NT + 3)
                    nc.vector.tensor_tensor(KV[:, t, D:2 * D], psG[:, DC:4, :].rearrange("p a b -> p (a b)"),
                                            bv[:, :], ALU.add).then_inc(S["v_ready"], 1)
                if has_s(T):
                    dve.wait_ge(S["fqk"], m + 1)
                    nc.vector.tensor_reduce(lg[:, NEAR:NO, :],
                                            fqk[:, :, :].rearrange("p o (h d) -> p (o h) d", d=HD),
                                            AX.X, ALU.add).then_inc(S["far_lg"], 1)
                    dve.wait_ge(S["far_lg"], m + 1)
                    dve.wait_ge(S["qs1"], m + 1)
                    dve.wait_ge(S[f"near{mp}"], dma_count(m, mt))
                    flat = lambda a: a.rearrange("p o h -> p (o h)")
                    l, e = flat(lg[:, :, :]), flat(ex[:, mp, :, :])
                    nc.vector.tensor_tensor(flat(qs1[:, mp, :, :]), l, flat(qs1[:, mp, :, :]), ALU.mult)\
                        .then_inc(S["prod"], 1)
                    dve.wait_ge(S["prod"], m + 1)
                    nc.vector.tensor_tensor(l, flat(qs1[:, mp, :, :]), bias[:, min(mt, BIAS_TILES - 1), :],
                                            ALU.add).then_inc(S["biased"], 1)
                    dve.wait_ge(S["biased"], m + 1)
                    nc.vector.tensor_reduce(mx[:, mp, :], lg[:, :, :].rearrange("p o h -> p h o"),
                                            AX.X, ALU.max).then_inc(S["mx"], 1)
                    dve.wait_ge(S["mx"], m + 1)
                    if there(m - 2):
                        dve.wait_ge(S[f"p_stored{mp}"], dma_count(m, mt))
                    wait(dve, S["fpv"], m - 1)
                    nc.vector.tensor_tensor(ex[:, mp, :, :], lg[:, :, :],
                                            mx[:, mp, :].unsqueeze(1).to_broadcast([P, NO, H]), ALU.subtract)\
                        .then_inc(S["shifted"], 1)
                if has_v(T):
                    dve.wait_ge(S["out_ps"], j + 1)
                    nc.vector.tensor_tensor(res[:, :], psO[:, DC:4, :].rearrange("p a b -> p (a b)"), ob[:, :],
                                            ALU.add).then_inc(S["res"], 1)
                    dve.wait_ge(S["res"], j + 1)
                    nc.vector.tensor_tensor(X[:, j, :], X[:, j, :], res[:, :], ALU.add).then_inc(S["x_new"], 1)
                if has_s(T):
                    dve.wait_ge(S["ex"], m + 1)
                    nc.vector.tensor_reduce(sm[:, mp, :], ex[:, mp, :, :].rearrange("p o h -> p h o"),
                                            AX.X, ALU.add).then_inc(S["sm"], 1)
                    dve.wait_ge(S["sm"], m + 1)
                    nc.vector.reciprocal(rs[:, mp, :], sm[:, mp, :]).then_inc(S["rs"], 1)
                    dve.wait_ge(S["rs"], m + 1)
                    nc.vector.tensor_tensor(ex[:, mp, :, :], ex[:, mp, :, :],
                                            rs[:, mp, :].unsqueeze(1).to_broadcast([P, NO, H]), ALU.mult)\
                        .then_inc(S["p_ready"], 1)

            rows(dve, step)

        @block.gpsimd
        def _(pool):
            nc.gpsimd.memset(pd[:, :, :], 0.0).then_inc(S["zeros"], 1)
            for buf in (KV[:, :, :], S64[:, :, :], S48[:, :, :], S96[:, :, :], kbd[:, 1, :, :, :], vp[:, :, :, :, :]):
                last = nc.gpsimd.memset(buf, 0.0)
            last.then_inc(S["zeros"], 1)
            pool.wait_ge(S["weights"], 16 * 14)
            pool.wait_ge(S["zeros"], 2)

            def sources(mt):
                return [S48[:, mt % 2, :], S64[:, mt % 4, :], S96[:, mt % 2, :], KV[:, (mt - 1) % NT, :],
                        S64[:, (mt - 1) % 4, :], KV[:, (mt - 2) % NT, :], KV[:, (mt - 3) % NT, :]]

            def step(T, t, first):
                par = t % 2
                m, mt = T - LAG_S, (t - LAG_S) % NT
                mp = mt % 2
                if has_s(T):
                    pool.wait_ge(S["qtok"], m + 1)
                    for name in ("shift48", "shift64", "shift96"):
                        pool.wait_ge(S[name], (m + 1) * 32)
                    wait(pool, S["far_lg"], m)
                    for o, src in enumerate(sources(mt)):
                        last = nc.gpsimd.tensor_tensor(fqk[:, o, :], qtok[:, mp, :], src[:, 0:D], ALU.mult)
                    last.then_inc(S["fqk"], 1)
                if first:
                    pool.wait_ge(S["kT"], T + 1)
                    wait(pool, S["s_ps"], T - 1 + 1)
                    nc.gpsimd.tensor_tensor(kbd[:, par, 0, :, :],
                                            kT[:, 0, :].unsqueeze(2).to_broadcast([P, P, HC]),
                                            hm[:, :].unsqueeze(1).to_broadcast([P, P, HC]), ALU.mult)\
                        .then_inc(S["kbd0"], 1)
                if has_w(T):
                    w, wt = T - LAG_W, (t - LAG_W) % NT
                    pool.wait_ge(S["vrep"], (w + 1) * 64)
                    wait(pool, S["o_ps"], w - 1)
                    nc.gpsimd.tensor_tensor(vh[:, wt % 2, :, :, :].rearrange("p g a d -> p g (a d)"),
                                            vrep[:, :].rearrange("p (g x) -> p g x", g=H // 4),
                                            qm[:, :, :].rearrange("p a d -> p (a d)").unsqueeze(1)
                                            .to_broadcast([P, H // 4, 4 * HD]), ALU.mult).then_inc(S["vh"], 1)
                if has_s(T):
                    pool.wait_ge(S["p_ready"], m + 1)
                    wait(pool, S["ftok"], m)
                    for o, src in enumerate(sources(mt)):
                        last = nc.gpsimd.tensor_tensor(
                            fpv[:, o, :].rearrange("p (h d) -> p h d", d=HD),
                            src[:, D:2 * D].rearrange("p (h d) -> p h d", d=HD),
                            ex[:, mp, NEAR + o, :].unsqueeze(2).to_broadcast([P, H, HD]), ALU.mult)
                    last.then_inc(S["fpv"], 1)

            rows(pool, step)

        @block.scalar
        def _(act):
            act.wait_ge(S["scaled"], DC + 1)
            act.wait_ge(S["zeros"], 2)
            act.wait_ge(S["biases"], BIAS_TILES)

            def step(T, t, first):
                par = t % 2
                m, mt = T - LAG_S, (t - LAG_S) % NT
                mp = mt % 2
                j = T - LAG_V
                if has_v(T):
                    act.wait_ge(S[f"band{(t - LAG_V) % 2}"], dma_count(j, (t - LAG_V) % NT, NSUB))
                    wait(act, S["pt_halo_ps"], j)
                    nc.scalar.activation(ph[:, :, :], pd[0:SUB, 0:SUB, :].rearrange("p k h -> p h k"), ACT.Copy)\
                        .then_inc(S["ph"], 1)
                    for g in range(4):
                        n = 4 * j + g
                        act.wait_ge(S["pt_ps"], n + 1)
                        wait(act, S["pv_used"], n - 1)
                        nc.scalar.activation(pT[:, g % 2, :, :], psT[:, g % 2, :, :], ACT.Copy).then_inc(S["pT"], 1)
                    act.wait_ge(S["pt_halo_ps"], j + 1)
                    wait(act, S["o_ps"], j)
                    nc.scalar.activation(phT[:, :, :], psT[:, 0, :, 0:SUB], ACT.Copy).then_inc(S["phT"], 1)
                if first:
                    act.wait_ge(S["xT_ps"], T + 1)
                    wait(act, S["gv_ps"], T)
                    nc.scalar.activation(xT[:, :, :], psX[:, 0:DC, :], ACT.Copy).then_inc(S["xT"], 1)
                    act.wait_ge(S["v_ready"], T + 1)
                    wait(act, S["at"], T + 1 - 4)
                    for c in range(DC):
                        last = nc.scalar.activation(gate[:, t % 4, c, :], psG[:, c, :], ACT.Tanh,
                                                    bias=bg[:, c:c + 1], scale=0.5)
                    last.then_inc(S["gate"], 1)
                    act.wait_ge(S["tok_ps"], T + 1)
                    wait(act, S["fqk"], T - 1)
                    nc.scalar.activation(qtok[:, par, :], psX[:, 0:DC, :].rearrange("p a b -> p (a b)"), ACT.Copy,
                                         scale=HD ** -0.5).then_inc(S["qtok"], 1)
                    wait(act, S["fqk"], T + 1 - NT + 3)
                    nc.scalar.activation(KV[:, t, 0:D], psX[:, DC:4, :].rearrange("p a b -> p (a b)"), ACT.Copy)\
                        .then_inc(S["ktok"], 1)
                    act.wait_ge(S["kT"], T + 1)
                    wait(act, S["s_ps"], T)
                    for h in range(HC):
                        last = nc.scalar.activation(kbd[:, par, 1, :, h], kT[:, 1, :], ACT.Copy,
                                                    scale=hm[:, h:h + 1])
                    last.then_inc(S["kbd1"], 1)
                    act.wait_ge(S["qs_ps"], T + 1)
                    wait(act, S["biased"], T - 1)
                    nc.scalar.activation(qs1[:, par, :, :].rearrange("p o (c h) -> p c o h", c=DC),
                                         psS[:, :, 0:NO * HC].rearrange("p c (o h) -> p c o h", h=HC),
                                         ACT.Copy, bias=1.0).then_inc(S["qs1"], 1)
                    act.wait_ge(S["s_ps"], T + 1)
                    if there(T - 1):
                        act.wait_ge(S[f"s_stored{1 - par}"], dma_count(T - 1, (t - 1) % NT))
                    nc.scalar.activation(ssb[:, :, :].rearrange("p k (c h) -> p c k h", c=DC),
                                         psS[:, :, :].rearrange("p c (k h) -> p c k h", h=HC),
                                         ACT.Copy, scale=HD ** -0.5).then_inc(S["ssb"], 1)
                if has_w(T):
                    w, wt = T - LAG_W, (t - LAG_W) % NT
                    act.wait_ge(S["v_ready"], w + 1)
                    wait(act, S["o_ps"], w - 1)
                    v = KV[:, wt, D:2 * D].rearrange("p (g a d) -> p g a d", a=2, d=HD)
                    for a in range(2):
                        last = nc.scalar.activation(vp[:, wt % 2, :, a, HD * a:HD * (a + 1)], v[:, :, a, :], ACT.Copy)
                    last.then_inc(S["vp"], 1)
                if has_s(T):
                    act.wait_ge(S["shifted"], m + 1)
                    e = ex[:, mp, :, :].rearrange("p o h -> p (o h)")
                    nc.scalar.activation(e, e, ACT.Exp).then_inc(S["ex"], 1)

            rows(act, step)

        @block.tensor
        def _(pe):
            pe.wait_ge(S["weights"], 16 * 14)
            pe.wait_ge(S["scaled"], DC)
            pe.wait_ge(S["zeros"], 2)

            def step(T, t, first):
                par = t % 2
                j, jt = T - LAG_V, (t - LAG_V) % NT
                jp = jt % 2
                if has_v(T):
                    def transpose_heads(g):
                        n = 4 * j + g
                        wait(pe, S["pT"], n - 1)
                        if g == 0:
                            wait(pe, S["phT"], j)
                        for a in range(4):
                            last = nc.tensor.transpose(psT[:, g % 2, a, :], pd[:, SUB:KEYS, 4 * g + a], ident[:, :])
                        last.then_inc(S["pt_ps"], 1)

                    def values(g):
                        pe.wait_ge(S["pT"], 4 * j + g + 1)
                        for a in range(4):
                            h = 4 * g + a
                            r = (h // 2 % 4) * 2 * HD
                            last = nc.tensor.matmul(psO[r:r + 2 * HD, g // 2, :], vp[:, jt % 2, h // 2, a % 2, :],
                                                    pT[:, g % 2, a, :], start=False, stop=False,
                                                    skip_group_check=True)
                        last.then_inc(S["pv_used"], 1)

                    def open_chunk(c):
                        nc.tensor.matmul(psO[:, c, :], ftok[:, jt % 2, c * P:(c + 1) * P], ident[:, :],
                                         start=True, stop=False, skip_group_check=True)

                    def close_chunk(c):
                        for g in (2 * c, 2 * c + 1):
                            last = nc.tensor.matmul(psO[64 * (g % 2):64 * (g % 2) + 64, c, 0:SUB],
                                                    vh[:, jt % 2, g, :, :].rearrange("p a d -> p (a d)"), phT[:, g, :],
                                                    start=False, stop=True, skip_group_check=True)
                        return last

                    pe.wait_ge(S[f"band{jp}"], dma_count(j, jt, NSUB))
                    transpose_heads(0)
                    transpose_heads(1)
                    pe.wait_ge(S["ftok"], j + 1)
                    pe.wait_ge(S["vp"], j + 1)
                    pe.wait_ge(S["vh"], j + 1)
                    wait(pe, S["res"], j)
                    open_chunk(0)
                    values(0)
                    transpose_heads(2)
                    values(1)
                    transpose_heads(3)
                    waits(pe, S["passed"], (S["pT"], 4 * j + 3), (S["ph"], j + 1))
                    for g in range(4):
                        last = nc.tensor.transpose(
                            psT[:, 0, g, 0:SUB],
                            ph[:, 4 * g:4 * g + 4, :].rearrange("p h k -> p (h k)"), ident[0:SUB, 0:SUB])
                    last.then_inc(S["pt_halo_ps"], 1)
                    pe.wait_ge(S["phT"], j + 1)
                    close_chunk(0)
                    open_chunk(1)
                    values(2)
                    values(3)
                    close_chunk(1).then_inc(S["o_ps"], 1)
                if first:
                    pe.wait_ge(S["xn"], T + 1)
                    wait(pe, S["ktok"], T)
                    for c in range(DC):
                        last = nc.tensor.transpose(psX[:, c, :], xn[:, c * P:(c + 1) * P], ident[:, :])
                    last.then_inc(S["xT_ps"], 1)
                    pe.wait_ge(S["xT"], T + 1)
                    wait(pe, S["kT"], T)
                    for e in range(2 * DC):
                        for c in range(DC):
                            last = nc.tensor.matmul(psP[:, e, :], wqkv[:, c, e * P:(e + 1) * P], xT[:, c, :],
                                                    start=(c == 0), stop=(c == DC - 1))
                    last.then_inc(S["qk_ps"], 1)
                if has_v(T):
                    pe.wait_ge(S["at"], j + 1)
                    for c in range(DC):
                        last = nc.tensor.matmul(psO[:, DC:4, :].rearrange("p a b -> p (a b)"), at[:, c, :],
                                                wo[:, c, :], start=(c == 0), stop=(c == DC - 1))
                    last.then_inc(S["out_ps"], 1)
                if first:
                    wait(pe, S["gate"], T)
                    for c in range(DC):
                        nc.tensor.matmul(psG[:, DC:4, :].rearrange("p a b -> p (a b)"), xT[:, c, :],
                                         wqkv[:, c, 2 * D:3 * D], start=(c == 0), stop=(c == DC - 1))
                    for e in range(DC):
                        for c in range(DC):
                            last = nc.tensor.matmul(psG[:, e, :], wg[:, c, e * P:(e + 1) * P], xT[:, c, :],
                                                    start=(c == 0), stop=(c == DC - 1))
                    last.then_inc(S["gv_ps"], 1)
                    pe.wait_ge(S["qT"], T + 1)
                    pe.wait_ge(S["kT"], T + 1)
                    for c in range(DC):
                        nc.tensor.transpose(psX[:, c, :], qT[:, c, :], ident[:, :])
                    for c in range(DC):
                        last = nc.tensor.transpose(psX[:, DC + c, :], kT[:, c, :], ident[:, :])
                    last.then_inc(S["tok_ps"], 1)
                    wait(pe, S["ssb"], T)
                    for c in range(DC):
                        last = nc.tensor.matmul(psS[:, c, 0:NO * HC], qT[:, c, :], se[:, :], start=True, stop=True)
                    last.then_inc(S["qs_ps"], 1)
                    pe.wait_ge(S["kbd0"], T + 1)
                    pe.wait_ge(S["kbd1"], T + 1)
                    pe.wait_ge(S["qs1"], T + 1)
                    for c in range(DC):
                        for s in range(NSUB):
                            r = slice(SUB * s, SUB * (s + 1))
                            q = qT[:, c, r]
                            flat = lambda a: a.rearrange("p k h -> p (k h)")
                            if s == 0:
                                nc.tensor.matmul(psS[r, c, 0:SUB * HC], q, flat(kbd[:, 1 - par, c, P - SUB:P, :]),
                                                 start=True, stop=True)
                                last = nc.tensor.matmul(psS[r, c, SUB * HC:WIN * HC], q, flat(kbd[:, par, c, 0:SUB, :]),
                                                        start=True, stop=True)
                            else:
                                k0 = SUB * (s - 1)
                                last = nc.tensor.matmul(psS[r, c, :], q, flat(kbd[:, par, c, k0:k0 + WIN, :]),
                                                        start=True, stop=True)
                    last.then_inc(S["s_ps"], 1)

            rows(pe, step)


def macaron(nc, x, x_out, s_dram, p_dram, c):
    with ExitStack() as ctx:
        X = ctx.enter_context(nc.sbuf_tensor("X", [P, TILES, D], F32))
        mean_all = ctx.enter_context(nc.sbuf_tensor("mean_all", [P, TILES], F32))
        rstd_all = ctx.enter_context(nc.sbuf_tensor("rstd_all", [P, TILES], F32))
        ffn = (c["w_r"], c["w_k"], c["w_v"], c["mu_r"], c["mu_k"], c["ident"])
        ffn_phase(nc, X, x, None, *ffn, "f0_", (mean_all, rstd_all))
        attention_phase(nc, X, mean_all, rstd_all, c["w_qkv"], c["w_gate"], c["w_out"], c["qk_bias"], c["v_bias"],
                        c["gate_bias"], c["out_bias"], c["gain"], c["scale_rows"], c["pos_rows"], c["masks"],
                        c["ident"], c["head_mask"], c["quad_mask"], s_dram, p_dram)
        ffn_phase(nc, X, None, x_out, *ffn, "f1_", None)


def kernel(**inputs):
    import numpy as np
    import concourse.bacc as bacc
    from concourse.bass_utils import run_bass_kernel_spmd

    a = {k.replace("L0_", ""): np.asarray(v) for k, v in inputs.items()}
    f32 = np.float32
    order = list(range(NEAR - 1, -1, -1)) + list(range(NEAR, NO))

    def columns(v):
        return v.reshape(-1, P).T

    scale_rows = np.zeros((HC, HD, NO, HC), f32)
    for h in range(HC):
        scale_rows[h, :, :, h] = a["attn_scale_embed"][order].T
    offsets = np.array(list(range(NEAR - 1, -1, -1)) + FAR)
    masks = np.zeros((P, NO, BIAS_TILES), f32)
    for t in range(BIAS_TILES):
        masks[:, :, t] = np.where(np.arange(P)[:, None] + P * t >= offsets[None, :], 0.0, -1e30)
    row = np.arange(P)
    arrays = {
        "x": a["attn_x"].reshape(B * N, D),
        "w_r": a["ffn_W_r"].T, "w_k": a["ffn_W_k"].T, "w_v": a["ffn_W_v"].T,
        "mu_r": columns(a["ffn_mu_r"]), "mu_k": columns(a["ffn_mu_k"]),
        "w_qkv": a["attn_qkv_w"].T, "w_gate": a["attn_gate_w"].T, "w_out": a["attn_out_w"].T,
        "qk_bias": columns(a["attn_qkv_b"][:2 * D]), "v_bias": a["attn_qkv_b"][2 * D:],
        "gate_bias": columns(a["attn_gate_b"]), "out_bias": a["attn_out_b"],
        "gain": columns(np.repeat(a["attn_if_gain"], HD)),
        "scale_rows": scale_rows.reshape(P, NO * HC), "pos_rows": a["attn_pos_bias"][order].reshape(-1),
        "masks": masks, "ident": np.eye(P, dtype=f32),
        "head_mask": (row[:, None] // HD == np.arange(HC)[None, :]).astype(f32),
        "quad_mask": np.repeat((row[:, None] // SUB == np.arange(4)[None, :]).astype(f32)[:, :, None], HD, axis=2),
    }
    arrays = {k: np.ascontiguousarray(v) for k, v in arrays.items()}
    nc = bacc.Bacc("TRN2", target_bir_lowering=False, num_devices=1)
    aps = {k: nc.dram_tensor(k, list(v.shape), F32, kind="ExternalInput").ap() for k, v in arrays.items()}
    out = nc.dram_tensor("out", [B * N, D], F32, kind="ExternalOutput").ap()
    s_dram = [nc.dram_tensor(f"s_scratch{i}", [P * WIN * H], F32, kind="Internal").ap() for i in range(2)]
    p_dram = [nc.dram_tensor(f"p_scratch{i}", [P * WIN * H], F32, kind="Internal").ap() for i in range(2)]
    x = aps.pop("x")
    macaron(nc, x, out, s_dram, p_dram, aps)
    r = run_bass_kernel_spmd(nc, [arrays], core_ids=[0])
    return r.results[0]["out"].reshape(B, N, D)
```

```python
import concourse.bass as bass
from concourse import mybir
from contextlib import ExitStack

F32 = mybir.dt.float32
ALU = mybir.AluOpType
ACT = mybir.ActivationFunctionType
AX = mybir.AxisListType

P = 128
B, N, D, H = 8, 1024, 256, 16
HD = D // H
DC = D // P
HC = H // DC
NT = N // P
TILES = B * NT
EPS = 1e-5

NEAR = 33
SUB = 32
WIN = 2 * SUB
NSUB = P // SUB
FAR = [48, 64, 96, 128, 192, 256, 384]
NO = NEAR + len(FAR)
NF = len(FAR)
LOC = NEAR * H
ALL = NO * H
MASKED = FAR[-1] // P
GROUP = 4
NG = TILES // GROUP
LAG_P, LAG_S, LAG_M, LAG_F, LAG_W, LAG_V, LAG_O = 1, 2, 3, 4, 4, 5, 6


def wait(eng, sem, value):
    if isinstance(value, int) and value <= 0:
        return
    eng.wait_ge(sem, value)


def waits(eng, passed, *pairs):
    for sem, value in pairs:
        if isinstance(value, int) and value <= 0:
            continue
        eng.wait_ge(sem, value).then_inc(passed, 1)


def ffn_phase(nc, X, x_in, out, w_r, w_k, w_v, mu_r, mu_k, ident_in, tag, stats_after):
    ctx = ExitStack()
    with ctx:
        def sb(name, shape):
            return ctx.enter_context(nc.sbuf_tensor(tag + name, shape, F32))

        def pb(name, shape):
            return ctx.enter_context(nc.psum_tensor(tag + name, shape, F32))

        def sem(name):
            return ctx.enter_context(nc.semaphore(tag + name))

        GT = GROUP * P
        wr = sb("wr", [P, DC, D])
        wk = sb("wk", [P, DC, D])
        wv = sb("wv", [P, DC, D])
        mur = sb("mur", [P, DC])
        muk = sb("muk", [P, DC])
        ident = sb("ident", [P, P])
        mhalf = sb("mhalf", [P, GROUP])
        st = sb("st", [P, 2, GROUP, 6])
        mv = sb("mv", [P, 2, GROUP, 2])
        ve = sb("ve", [P, 2, GROUP])
        rstd = sb("rstd", [P, 2, GROUP])
        xn = sb("xn", [P, 2, GROUP, D])
        xT = sb("xT", [P, 2, DC, 1 + GT])
        dx = sb("dx", [P, 2, DC, GT])
        xr = sb("xr", [P, 2, DC, GT])
        xk = sb("xk", [P, 2, DC, GT])
        kr = sb("kr", [P, DC, GT])
        ka = sb("ka", [P, 2, DC, GT])
        th = sb("th", [P, 2, GROUP, D])
        rv = sb("rv", [P, 2, GROUP, D])
        st2 = sb("st2", [P, 2, GROUP, 6])
        mv2 = sb("mv2", [P, 2, GROUP, 2])
        ve2 = sb("ve2", [P, 2, GROUP])

        psT = pb("psT", [P, DC, GT])
        psK = pb("psK", [P, DC, GT])
        psR = pb("psR", [P, GROUP, D])
        psV = pb("psV", [P, GROUP, D])

        s_w = sem("weights_loaded")
        s_x = sem("x_loaded")
        s_c = sem("constants_set")
        s_st = sem("stats_of_tile")
        s_mv = sem("mean_var_of_tile")
        s_ve = sem("var_plus_eps")
        s_rs = sem("rstd_ready")
        s_xn = sem("xn_ready")
        s_T = sem("transposed_in_psum")
        s_xT = sem("xT_ready")
        s_dx = sem("dx_ready")
        s_mix = sem("mixed_ready")
        s_K = sem("k_in_psum")
        s_kr = sem("relu_done")
        s_ka = sem("squared_ready")
        s_R = sem("r_in_psum")
        s_th = sem("tanh_ready")
        s_V = sem("v_in_psum")
        s_rv = sem("rv_done")
        s_res = sem("residual_done")
        s_st2 = sem("new_stats")
        s_mv2 = sem("new_mean_var")
        s_ve2 = sem("new_var_plus_eps")
        s_rs2 = sem("new_rstd")
        s_out = sem("stored")
        s_passed = sem("waits_passed")

        block = ctx.enter_context(nc.Block())
        GB = NT // GROUP

        @block.sync
        def _(sp):
            sp.dma_start(wk[:, :, :], w_k.rearrange("(c p) n -> p c n", p=P)).then_inc(s_w, 16)
            sp.dma_start(wr[:, :, :], w_r.rearrange("(c p) n -> p c n", p=P)).then_inc(s_w, 16)
            sp.dma_start(wv[:, :, :], w_v.rearrange("(c p) n -> p c n", p=P)).then_inc(s_w, 16)
            sp.dma_start(ident[:, :], ident_in).then_inc(s_w, 16)
            sp.dma_start(mur[:, :], mu_r).then_inc(s_w, 16)
            sp.dma_start(muk[:, :], mu_k).then_inc(s_w, 16)
            if x_in is not None:
                xv = x_in.rearrange("(t p) d -> p t d", p=P)
                for g in range(NG):
                    wait(sp, s_x, 16 * g)
                    sp.dma_start(X[:, g * GROUP:(g + 1) * GROUP, :],
                                 xv[:, g * GROUP:(g + 1) * GROUP, :]).then_inc(s_x, 16)
            if out is not None:
                ov = out.rearrange("(t p) d -> p t d", p=P)
                for g in range(NG):
                    sp.wait_ge(s_res, GROUP * (g + 1))
                    sp.dma_start(ov[:, g * GROUP:(g + 1) * GROUP, :],
                                 X[:, g * GROUP:(g + 1) * GROUP, :]).then_inc(s_out, 16)
                sp.wait_ge(s_out, 16 * NG)
            sp.wait_ge(s_w, 96)

        @block.vector
        def _(dve):
            nc.vector.memset(mhalf[:, :], -0.5).then_inc(s_c, 1)
            nc.vector.memset(xT[:, 0, :, 0:1], 0.0).then_inc(s_c, 1)

            def norm(G, par):
                if x_in is not None:
                    waits(dve, s_passed, (s_x, 16 * (G + 1)))
                for u in range(GROUP):
                    nc.vector.bn_stats(st[:, par, u, :], X[:, G * GROUP + u, :]).then_inc(s_st, 1)
                for u in range(GROUP):
                    waits(dve, s_passed, (s_st, GROUP * G + u + 1))
                    nc.vector.bn_aggr(mv[:, par, u, :], st[:, par, u, :]).then_inc(s_mv, 1)
                dve.wait_ge(s_mv, GROUP * (G + 1))
                nc.vector.tensor_scalar(ve[:, par, :], mv[:, par, :, 1], EPS, None, ALU.add).then_inc(s_ve, 1)
                dve.wait_ge(s_rs, G + 1)
                wait(dve, s_T, G - 1)
                for u in range(GROUP):
                    last = nc.vector.tensor_scalar(xn[:, par, u, :], X[:, G * GROUP + u, :],
                                                   mv[:, par, u, 0:1], rstd[:, par, u:u + 1],
                                                   ALU.subtract, ALU.mult)
                last.then_inc(s_xn, 1)

            def mix(G, par):
                dve.wait_ge(s_dx, G + 1)
                wait(dve, s_V, G - 1)
                for dst, mu in ((xk, muk), (xr, mur)):
                    for c in range(DC):
                        nc.vector.scalar_tensor_tensor(dst[:, par, c, :], dx[:, par, c, :], mu[:, c:c + 1],
                                                       xT[:, par, c, 0:GT], ALU.mult, ALU.add).then_inc(s_mix, 1)

            def final(G, par):
                dve.wait_ge(s_th, G + 1)
                dve.wait_ge(s_V, G + 1)
                for u in range(GROUP):
                    nc.vector.scalar_tensor_tensor(rv[:, par, u, :], th[:, par, u, :], 1.0, psV[:, u, :],
                                                   ALU.add, ALU.mult).then_inc(s_rv, 1)
                for u in range(GROUP):
                    dve.wait_ge(s_rv, GROUP * G + u + 1)
                    x = X[:, G * GROUP + u, :]
                    nc.vector.scalar_tensor_tensor(x, rv[:, par, u, :], 0.25, x,
                                                   ALU.mult, ALU.add).then_inc(s_res, 1)
                if stats_after is None:
                    return
                for u in range(GROUP):
                    waits(dve, s_passed, (s_res, GROUP * G + u + 1))
                    nc.vector.bn_stats(st2[:, par, u, :], X[:, G * GROUP + u, :]).then_inc(s_st2, 1)
                waits(dve, s_passed, (s_rs2, 2 * (G - 1)))
                for u in range(GROUP):
                    waits(dve, s_passed, (s_st2, GROUP * G + u + 1))
                    nc.vector.bn_aggr(mv2[:, par, u, :], st2[:, par, u, :]).then_inc(s_mv2, 1)
                dve.wait_ge(s_mv2, GROUP * (G + 1))
                nc.vector.tensor_scalar(ve2[:, par, :], mv2[:, par, :, 1], EPS, None, ALU.add).then_inc(s_ve2, 1)

            dve.wait_ge(s_w, 96)
            dve.wait_ge(s_c, 2)
            norm(0, 0)
            norm(1, 1)
            mix(0, 0)

            def ahead(G, g):
                norm(G + 2, g)
                mix(G + 1, 1 - g)
                final(G, g)

            for g in range(GB):
                ahead(g, g)
            with dve.Fori(1, B - 1) as b:
                for g in range(GB):
                    ahead(b * GB + g, g)
            mix(NG - 1, 1)
            final(NG - 2, 0)
            final(NG - 1, 1)

        @block.gpsimd
        def _(pool):
            pool.wait_ge(s_c, 2)

            def rs(G, par):
                pool.wait_ge(s_ve, G + 1)
                wait(pool, s_xn, G - 1)
                nc.gpsimd.tensor_tensor(rstd[:, par, :], ve[:, par, :], mhalf[:, :], ALU.pow).then_inc(s_rs, 1)

            def diff(G, par):
                pool.wait_ge(s_xT, G + 1)
                wait(pool, s_mix, 2 * DC * (G - 1))
                nc.gpsimd.tensor_tensor(dx[:, par, :, :], xT[:, par, :, 1:1 + GT], xT[:, par, :, 0:GT],
                                        ALU.subtract).then_inc(s_dx, 1)

            def new(G, par):
                if stats_after is None:
                    return
                mean_all, rstd_all = stats_after
                pool.wait_ge(s_ve2, G + 1)
                nc.gpsimd.tensor_copy(mean_all[:, bass.ds(G * GROUP, GROUP)], mv2[:, par, :, 0]).then_inc(s_rs2, 1)
                nc.gpsimd.tensor_tensor(rstd_all[:, bass.ds(G * GROUP, GROUP)], ve2[:, par, :], mhalf[:, :],
                                        ALU.pow).then_inc(s_rs2, 1)

            rs(0, 0)
            rs(1, 1)
            diff(0, 0)
            def ahead(G, g):
                rs(G + 2, g)
                diff(G + 1, 1 - g)
                new(G, g)

            for g in range(GB):
                ahead(g, g)
            with pool.Fori(1, B - 1) as b:
                for g in range(GB):
                    ahead(b * GB + g, g)
            diff(NG - 1, 1)
            new(NG - 2, 0)
            new(NG - 1, 1)

        @block.scalar
        def _(act):
            def xt(G, par):
                act.wait_ge(s_T, G + 1)
                wait(act, s_mix, 2 * DC * (G - 1))
                last = nc.scalar.activation(xT[:, par, :, 1:1 + GT], psT[:, :, :], ACT.Copy)
                if par:
                    act.wait_ge(s_xT, G)
                    last = nc.scalar.activation(xT[:, 1, :, 0:1], xT[:, 0, :, GT:GT + 1], ACT.Copy)
                last.then_inc(s_xT, 1)

            def rest(G, par):
                act.wait_ge(s_K, G + 1)
                wait(act, s_ka, G)
                nc.scalar.activation(kr[:, :, :], psK[:, :, :], ACT.Relu).then_inc(s_kr, 1)
                act.wait_ge(s_kr, G + 1)
                wait(act, s_V, G - 1)
                nc.scalar.activation(ka[:, par, :, :], kr[:, :, :], ACT.Square).then_inc(s_ka, 1)
                act.wait_ge(s_R, G + 1)
                wait(act, s_rv, GROUP * (G - 1))
                nc.scalar.activation(th[:, par, :, :], psR[:, :, :], ACT.Tanh, scale=0.5).then_inc(s_th, 1)

            xt(0, 0)
            def ahead(G, g):
                xt(G + 1, 1 - g)
                rest(G, g)

            for g in range(GB):
                ahead(g, g)
            with act.Fori(1, B - 1) as b:
                for g in range(GB):
                    ahead(b * GB + g, g)
            xt(NG - 1, 1)
            rest(NG - 2, 0)
            rest(NG - 1, 1)

        @block.tensor
        def _(pe):
            def tr(G, par):
                pe.wait_ge(s_xn, G + 1)
                wait(pe, s_xT, G)
                for c in range(DC):
                    for u in range(GROUP):
                        last = nc.tensor.transpose(psT[:, c, u * P:(u + 1) * P], xn[:, par, u, c * P:(c + 1) * P],
                                                   ident[:, :])
                last.then_inc(s_T, 1)

            def products(G, par):
                pe.wait_ge(s_mix, 2 * DC * G + DC)
                wait(pe, s_kr, G)
                for e in range(DC):
                    for c in range(DC):
                        last = nc.tensor.matmul(psK[:, e, :], wk[:, c, e * P:(e + 1) * P], xk[:, par, c, :],
                                                start=(c == 0), stop=(c == DC - 1))
                last.then_inc(s_K, 1)
                pe.wait_ge(s_mix, 2 * DC * (G + 1))
                wait(pe, s_th, G)
                for u in range(GROUP):
                    for c in range(DC):
                        last = nc.tensor.matmul(psR[:, u, :], xr[:, par, c, u * P:(u + 1) * P], wr[:, c, :],
                                                start=(c == 0), stop=(c == DC - 1))
                last.then_inc(s_R, 1)
                pe.wait_ge(s_ka, G + 1)
                wait(pe, s_rv, GROUP * G)
                for u in range(GROUP):
                    for c in range(DC):
                        last = nc.tensor.matmul(psV[:, u, :], ka[:, par, c, u * P:(u + 1) * P], wv[:, c, :],
                                                start=(c == 0), stop=(c == DC - 1))
                last.then_inc(s_V, 1)

            pe.wait_ge(s_w, 96)
            tr(0, 0)
            def ahead(G, g):
                tr(G + 1, 1 - g)
                products(G, g)

            for g in range(GB):
                ahead(g, g)
            with pe.Fori(1, B - 1) as b:
                for g in range(GB):
                    ahead(b * GB + g, g)
            tr(NG - 1, 1)
            products(NG - 2, 0)
            products(NG - 1, 1)


def attention_phase(nc, X, mean_all, rstd_all, w_qkv, w_gate, w_out, qkv_bias, gate_bias, out_bias,
                    gain, scale_rows, pos_rows, masks, ident_in, head_mask, s_dram, p_dram):
    ctx = ExitStack()
    with ctx:
        def sb(name, shape):
            return ctx.enter_context(nc.sbuf_tensor("a_" + name, shape, F32))

        def pb(name, shape):
            return ctx.enter_context(nc.psum_tensor("a_" + name, shape, F32))

        def sem(name):
            return ctx.enter_context(nc.semaphore("a_" + name))

        KEYS = SUB + P
        wqkv = sb("wqkv", [P, DC, 3 * D])
        wg = sb("wg", [P, DC, D])
        wo = sb("wo", [P, DC, D])
        bqkv = sb("bqkv", [P, 3 * D])
        bg = sb("bg", [P, DC])
        ob = sb("ob", [P, D])
        gn = sb("gn", [P, DC])
        se = sb("se", [P, NO * HC])
        ident = sb("ident", [P, P])
        hm = sb("hm", [P, HC])
        bias = sb("bias", [P, ALL])
        mask = sb("mask", [P, MASKED, NO])
        xn = sb("xn", [P, D])
        xT = sb("xT", [P, DC, P])
        qkT = sb("qkT", [P, 2, 2 * DC, P])
        kbd = sb("kbd", [P, 2, DC, P, HC])
        gtok = sb("gtok", [P, D])
        gate = sb("gate", [P, NT, DC, P])
        qtok = sb("qtok", [P, 2, D])
        KV = sb("KV", [P, NT, 2 * D])
        S64 = sb("S64", [P, 8, D])
        S48 = sb("S48", [P, 6, D])
        S96 = sb("S96", [P, 6, D])
        vp = sb("vp", [P, 2, H // 2, 2, 2 * HD])
        vh = sb("vh", [P, 2, H // 4, 4, HD])
        ssb = sb("ssb", [P, WIN, H])
        qs1 = sb("qs1", [P, NO, H])
        lg = sb("lg", [P, NO, H])
        ex = sb("ex", [P, 2, NO, H])
        mx = sb("mx", [P, H])
        sm = sb("sm", [P, H])
        rs = sb("rs", [P, H])
        fqk = sb("fqk", [P, NF, D])
        fpv = sb("fpv", [P, NF, D])
        ftok = sb("ftok", [P, 2, D])
        pd = sb("pd", [P, KEYS, H])
        ph = sb("ph", [SUB, H, SUB])
        pT = sb("pT", [P, 2, 4, P])
        phT = sb("phT", [P, 4, SUB])
        at = sb("at", [P, DC, P])

        psX = pb("psX", [P, 4, P])
        psP = pb("psP", [P, 4, P])
        psG = pb("psG", [P, 4, P])
        psS = pb("psS", [P, DC, 512])
        psT = pb("psT", [P, 2, 4, P])
        psO = pb("psO", [P, 4, P])

        names = """weights scaled zeros xn xT_ps xT pr_ps q_tok k_ready v_ready gtok qkT_ps qkT gT_ps gate
            moved0 moved1 vp vh kbd0 kbd1 qs_ps qs1 s_ps ssb s_stored0 s_stored1 near0 near1
            fqk far_lg prod biased masked mx shifted ex sm rs p_ready fpv ftok p_stored0 p_stored1 band0 band1
            pt_ps pt_halo_ps ph pv_used pT phT o_ps at out_ps with_out x_new passed sp_passed act_passed""".split()
        S = {n: sem(n) for n in names}
        LOADS = 12
        block = ctx.enter_context(nc.Block())

        def rows(eng, step):
            for t in range(NT):
                step(t, t)
            with eng.Fori(1, B) as b:
                for t in range(NT):
                    step(b * NT + t, t)
            for t in range(LAG_O):
                step(TILES + t, t)

        def stage(T, t, lag):
            return T - lag, (t - lag) % NT, not isinstance(T, int) or 0 <= T - lag < TILES

        def dma_count(T, t, per=1):
            return 16 * per * (T // 2 + 1) if isinstance(T, int) else (T - t) * (8 * per) + 16 * per * (t // 2 + 1)

        SHIFTED = ((48, S48, 2), (64, S64, 4), (96, S96, 2))
        ROW = WIN * H

        def band(dram):
            return bass.AP(dram.tensor, dram.offset, [[SUB * ROW, NSUB], [ROW + H, SUB], [1, LOC]])

        def by_rows(dram):
            return dram.rearrange("(p k) -> p k", p=P)

        def flat(a):
            return a.rearrange("p a b -> p (a b)")

        @block.sync
        def _(sp):
            loads = [(wqkv[:, :, :], w_qkv.rearrange("(c p) n -> p c n", p=P)),
                     (wg[:, :, :], w_gate.rearrange("(c p) n -> p c n", p=P)),
                     (wo[:, :, :], w_out.rearrange("(c p) n -> p c n", p=P)),
                     (bqkv[:, :], qkv_bias.partition_broadcast(P)), (bg[:, :], gate_bias), (gn[:, :], gain),
                     (ob[:, :], out_bias.partition_broadcast(P)),
                     (se[:, :], scale_rows), (ident[:, :], ident_in), (hm[:, :], head_mask),
                     (bias[:, :], pos_rows.partition_broadcast(P)), (mask[:, :, :], masks)]
            for dst, src in loads:
                sp.dma_start(dst, src).then_inc(S["weights"], 16)
            assert LOADS == len(loads)
            sp.wait_ge(S["zeros"], 1)
            for par in range(2):
                sp.dma_start(by_rows(p_dram[par]), flat(pd[:, 0:WIN, :])).then_inc(S[f"p_stored{par}"], 16)

            def step(T, t):
                i, it, there = stage(T, t, LAG_P)
                if there:
                    waits(sp, S["sp_passed"], (S["k_ready"], i + 1), (S["v_ready"], i + 1),
                          (S["fqk"], i - 1), (S["fpv"], i - 2))
                    for sh, buf, ks in SHIFTED:
                        k, v = it % ks, ks + it % 4
                        for dst, src in ((buf[0:sh], KV[P - sh:P, (it - 1) % NT, :]), (buf[sh:P], KV[0:P - sh, it, :])):
                            sp.dma_start(dst[:, k:v + 1:v - k, :], src.rearrange("p (a d) -> p a d", a=2))\
                                .then_inc(S[f"moved{it % 2}"], 16)
                m, mt, there = stage(T, t, LAG_M)
                if there:
                    mp = mt % 2
                    waits(sp, S["sp_passed"], (S["p_ready"], m + 1),
                          (S[f"band{mp}"], dma_count(m, mt, NSUB) - 16 * NSUB), (S[f"p_stored{mp}"], dma_count(m, mt)))
                    sp.dma_start(band(p_dram[mp]), flat(ex[:, mp, 0:NEAR, :])).then_inc(S[f"p_stored{mp}"], 16)
                w, wt, there = stage(T, t, LAG_W)
                if there:
                    waits(sp, S["sp_passed"], (S["pt_halo_ps"], w), (S[f"p_stored{wt % 2}"], dma_count(w, wt) + 16))
                    for s in range(NSUB):
                        sp.dma_start(flat(pd[SUB * s:SUB * (s + 1), SUB * s:SUB * s + WIN, :]),
                                     by_rows(p_dram[wt % 2])[SUB * s:SUB * (s + 1), :]).then_inc(S[f"band{wt % 2}"], 16)
                    waits(sp, S["sp_passed"], (S["o_ps"], w))
                    for j in range(4):
                        sp.dma_start(vh[SUB * j:SUB * (j + 1), wt % 2, :, j, :],
                                     KV[P - SUB:P, (wt - 1) % NT, D:2 * D]
                                     .rearrange("p (g a d) -> p g a d", a=4, d=HD)[:, :, j, :]).then_inc(S["vh"], 16)

            rows(sp, step)

        @block.vector
        def _(dve):
            dve.wait_ge(S["weights"], 16 * LOADS)
            scale = HD ** -0.5
            for c in range(DC):
                nc.vector.tensor_scalar(wo[:, c, :], wo[:, c, :], gn[:, c:c + 1], 0.5, ALU.mult, ALU.mult)\
                    .then_inc(S["scaled"], 1)
            for a, by in ((bg[:, :], 0.5), (wqkv[:, :, 0:D], scale), (bqkv[:, 0:D], scale), (se[:, :], 1 / scale)):
                nc.vector.tensor_scalar(a, a, by, None, ALU.mult).then_inc(S["scaled"], 1)
            dve.wait_ge(S["scaled"], DC + 4)
            dve.wait_ge(S["zeros"], 2)

            def normed(n):
                wait(dve, S["xT_ps"], n)
                nc.vector.tensor_scalar(xn[:, :], X[:, n, :], mean_all[:, bass.ds(n, 1)], rstd_all[:, bass.ds(n, 1)],
                                        ALU.subtract, ALU.mult).then_inc(S["xn"], 1)

            def step(T, t):
                n, nt, there_n = stage(T, t, 0)
                i, it, there_i = stage(T, t, LAG_P)
                m, mt, there_m = stage(T, t, LAG_M)
                mp = mt % 2
                o, ot, there_o = stage(T, t, LAG_O)
                if there_m:
                    dve.wait_ge(S["fqk"], m + 1)
                    nc.vector.tensor_reduce(lg[:, NEAR:NO, :], fqk[:, :, :].rearrange("p o (h d) -> p (o h) d", d=HD),
                                            AX.X, ALU.add).then_inc(S["far_lg"], 1)
                if there_o:
                    dve.wait_ge(S["o_ps"], o + 1)
                    wait(dve, S["out_ps"], o)
                    nc.vector.scalar_tensor_tensor(at[:, :, :], gate[:, ot, :, :], 1.0, psO[:, 0:DC, :],
                                                   ALU.add, ALU.mult).then_inc(S["at"], 1)
                if there_i:
                    dve.wait_ge(S["pr_ps"], i + 1)
                    wait(dve, S["fqk"], i - 1)
                    wait(dve, S["qkT_ps"], i - 1)
                    nc.vector.tensor_tensor(qtok[:, it % 2, :], flat(psP[:, 0:DC, :]), bqkv[:, 0:D], ALU.add)\
                        .then_inc(S["q_tok"], 1)
                    wait(dve, S["fpv"], i + 1 - NT + 3)
                    wait(dve, S["vh"], 64 * (i + 1 - NT + 1) if isinstance(i, int) else (i - NT + 2) * 64)
                    nc.vector.tensor_tensor(KV[:, it, 0:D], flat(psP[:, DC:4, :]), bqkv[:, D:2 * D], ALU.add)\
                        .then_inc(S["k_ready"], 1)
                    nc.vector.tensor_tensor(KV[:, it, D:2 * D], flat(psG[:, 0:DC, :]), bqkv[:, 2 * D:3 * D], ALU.add)\
                        .then_inc(S["v_ready"], 1)
                if there_m:
                    dve.wait_ge(S["far_lg"], m + 1)
                    dve.wait_ge(S["qs1"], m + 1)
                    dve.wait_ge(S[f"near{mp}"], dma_count(m, mt))
                    nc.vector.tensor_tensor(flat(lg[:, :, :]), flat(lg[:, :, :]), flat(qs1[:, :, :]), ALU.mult)\
                        .then_inc(S["prod"], 1)
                    dve.wait_ge(S["prod"], m + 1)
                    nc.vector.tensor_tensor(flat(lg[:, :, :]), flat(lg[:, :, :]), bias[:, :],
                                            ALU.add).then_inc(S["biased"], 1)
                    dve.wait_ge(S["biased"], m + 1)
                    if mt < MASKED:
                        o0 = 0 if mt == 0 else NEAR + min(k for k in range(NF) if FAR[k] >= P * mt)
                        rest = 1 if mt < MASKED - 1 else NT + 1 - MASKED
                        nc.vector.tensor_tensor(lg[:, o0:NO, :], lg[:, o0:NO, :],
                                                mask[:, mt, o0:NO].unsqueeze(2).to_broadcast([P, NO - o0, H]),
                                                ALU.add).then_inc(S["masked"], rest)
                        dve.wait_ge(S["masked"], m + rest)
                    nc.vector.tensor_reduce(mx[:, :], lg[:, :, :].rearrange("p o h -> p h o"),
                                            AX.X, ALU.max).then_inc(S["mx"], 1)
                    dve.wait_ge(S["mx"], m + 1)
                    dve.wait_ge(S[f"p_stored{mp}"], dma_count(m, mt))
                    wait(dve, S["fpv"], m - 1)
                    nc.vector.tensor_tensor(ex[:, mp, :, :], lg[:, :, :],
                                            mx[:, :].unsqueeze(1).to_broadcast([P, NO, H]), ALU.subtract)\
                        .then_inc(S["shifted"], 1)
                if there_o:
                    dve.wait_ge(S["out_ps"], o + 1)
                    nc.vector.tensor_tensor(X[:, o, :], flat(psO[:, DC:4, :]), X[:, o, :], ALU.add)\
                        .then_inc(S["with_out"], 1)
                    dve.wait_ge(S["with_out"], o + 1)
                    nc.vector.tensor_tensor(X[:, o, :], X[:, o, :], ob[:, :], ALU.add).then_inc(S["x_new"], 1)
                if there_n:
                    normed(n)
                if there_m:
                    dve.wait_ge(S["ex"], m + 1)
                    nc.vector.tensor_reduce(sm[:, :], ex[:, mp, :, :].rearrange("p o h -> p h o"),
                                            AX.X, ALU.add).then_inc(S["sm"], 1)
                    dve.wait_ge(S["sm"], m + 1)
                    nc.vector.reciprocal(rs[:, :], sm[:, :]).then_inc(S["rs"], 1)
                    dve.wait_ge(S["rs"], m + 1)
                    nc.vector.tensor_tensor(ex[:, mp, :, :], ex[:, mp, :, :],
                                            rs[:, :].unsqueeze(1).to_broadcast([P, NO, H]), ALU.mult)\
                        .then_inc(S["p_ready"], 1)
                f, ft, there = stage(T, t, LAG_F)
                if there:
                    dve.wait_ge(S["fpv"], f + 1)
                    wait(dve, S["o_ps"], f - 1)
                    nc.vector.tensor_reduce(ftok[:, ft % 2, :], fpv[:, :, :].rearrange("p o d -> p d o"),
                                            AX.X, ALU.add).then_inc(S["ftok"], 1)

            rows(dve, step)

        @block.gpsimd
        def _(pool):
            nc.gpsimd.memset(pd[:, :, :], 0.0).then_inc(S["zeros"], 1)
            for buf in (KV[:, :, :], S64[:, :, :], S48[:, :, :], S96[:, :, :], kbd[:, 1, :, :, :], vp[:, :, :, :, :],
                        vh[:, :, :, :, :]):
                last = nc.gpsimd.memset(buf, 0.0)
            last.then_inc(S["zeros"], 1)
            pool.wait_ge(S["weights"], 16 * LOADS)
            pool.wait_ge(S["zeros"], 2)

            def far_keys(t):
                return [S48[:, t % 2, :], S64[:, t % 4, :], S96[:, t % 2, :], KV[:, (t - 1) % NT, 0:D],
                        S64[:, (t - 1) % 4, :], KV[:, (t - 2) % NT, 0:D], KV[:, (t - 3) % NT, 0:D]]

            def far_values(t):
                return [S48[:, 2 + t % 4, :], S64[:, 4 + t % 4, :], S96[:, 2 + t % 4, :], KV[:, (t - 1) % NT, D:2 * D],
                        S64[:, 4 + (t - 1) % 4, :], KV[:, (t - 2) % NT, D:2 * D], KV[:, (t - 3) % NT, D:2 * D]]

            def step(T, t):
                f, ft, there = stage(T, t, LAG_F)
                if there:
                    pool.wait_ge(S["p_ready"], f + 1)
                    wait(pool, S["ftok"], f)
                    for o, src in enumerate(far_values(ft)):
                        last = nc.gpsimd.tensor_tensor(
                            fpv[:, o, :].rearrange("p (h d) -> p h d", d=HD),
                            src.rearrange("p (h d) -> p h d", d=HD),
                            ex[:, ft % 2, NEAR + o, :].unsqueeze(2).to_broadcast([P, H, HD]), ALU.mult)
                    last.then_inc(S["fpv"], 1)
                s, st, there = stage(T, t, LAG_S)
                if there:
                    pool.wait_ge(S["q_tok"], s + 1)
                    pool.wait_ge(S[f"moved{st % 2}"], dma_count(s, st, 2 * len(SHIFTED)))
                    wait(pool, S["far_lg"], s)
                    for o, src in enumerate(far_keys(st)):
                        last = nc.gpsimd.tensor_tensor(fqk[:, o, :], qtok[:, st % 2, :], src, ALU.mult)
                    last.then_inc(S["fqk"], 1)
                i, it, there = stage(T, t, LAG_P)
                if there:
                    pool.wait_ge(S["qkT"], i + 1)
                    wait(pool, S["s_ps"], i)
                    nc.gpsimd.tensor_tensor(kbd[:, it % 2, 0, :, :],
                                            qkT[:, it % 2, DC, :].unsqueeze(2).to_broadcast([P, P, HC]),
                                            hm[:, :].unsqueeze(1).to_broadcast([P, P, HC]), ALU.mult)\
                        .then_inc(S["kbd0"], 1)

            rows(pool, step)

        @block.scalar
        def _(act):
            act.wait_ge(S["scaled"], DC + 4)
            act.wait_ge(S["zeros"], 2)

            def x_transposed(n):
                act.wait_ge(S["xT_ps"], n + 1)
                wait(act, S["pr_ps"], n)
                nc.scalar.activation(xT[:, :, :], psX[:, 0:DC, :], ACT.Copy).then_inc(S["xT"], 1)

            def step(T, t):
                n, nt, there_n = stage(T, t, 0)
                i, it, there_i = stage(T, t, LAG_P)
                s, st, there_s = stage(T, t, LAG_S)
                m, mt, there_m = stage(T, t, LAG_M)
                w, wt, there_w = stage(T, t, LAG_W)
                j, jt, there_j = stage(T, t, LAG_V)
                if there_i:
                    act.wait_ge(S["v_ready"], i + 1)
                    wait(act, S["gT_ps"], i)
                    nc.scalar.activation(gtok[:, :], flat(psG[:, DC:4, :]), ACT.Copy).then_inc(S["gtok"], 1)
                if there_i:
                    act.wait_ge(S["qkT_ps"], i + 1)
                    wait(act, S["qs_ps"], i - 1)
                    wait(act, S["kbd0"], i - 1)
                    nc.scalar.activation(qkT[:, it % 2, :, :], psX[:, :, :], ACT.Copy).then_inc(S["qkT"], 1)
                if there_s:
                    act.wait_ge(S["qs_ps"], s + 1)
                    wait(act, S["prod"], s)
                    nc.scalar.activation(qs1[:, :, :].rearrange("p o (c h) -> p c o h", c=DC),
                                         psS[:, :, 0:NO * HC].rearrange("p c (o h) -> p c o h", h=HC),
                                         ACT.Copy, bias=1.0).then_inc(S["qs1"], 1)
                if there_j:
                    act.wait_ge(S[f"band{jt % 2}"], dma_count(j, jt, NSUB))
                    wait(act, S["pt_halo_ps"], j)
                    nc.scalar.activation(ph[:, :, :], pd[0:SUB, 0:SUB, :].rearrange("p k h -> p h k"), ACT.Copy)\
                        .then_inc(S["ph"], 1)

                def evacuate(g):
                    act.wait_ge(S["pt_ps"], 4 * j + g + 1)
                    wait(act, S["pv_used"], 4 * j + g - 1)
                    nc.scalar.activation(pT[:, g % 2, :, :], psT[:, g % 2, :, :], ACT.Copy).then_inc(S["pT"], 1)

                if there_j:
                    evacuate(0)
                    evacuate(1)
                if there_m:
                    act.wait_ge(S["shifted"], m + 1)
                    e = flat(ex[:, mt % 2, :, :])
                    nc.scalar.activation(e, e, ACT.Exp).then_inc(S["ex"], 1)
                if there_s:
                    act.wait_ge(S["s_ps"], s + 1)
                    if not isinstance(s, int) or s > 0:
                        act.wait_ge(S[f"s_stored{1 - st % 2}"], dma_count(s - 1, (st - 1) % NT))
                    nc.scalar.activation(ssb[:, :, :].rearrange("p k (c h) -> p c k h", c=DC),
                                         psS[:, :, :].rearrange("p c (k h) -> p c k h", h=HC),
                                         ACT.Copy).then_inc(S["ssb"], 1)
                if there_j:
                    evacuate(2)
                    evacuate(3)
                if there_s:
                    waits(act, S["act_passed"], (S["ssb"], s + 1),
                          (S[f"near{st % 2}"], dma_count(s, st) - 16))
                    act.dma_start(by_rows(s_dram[st % 2]), flat(ssb[:, :, :])).then_inc(S[f"s_stored{st % 2}"], 16)
                if there_j:
                    act.wait_ge(S["pt_halo_ps"], j + 1)
                    wait(act, S["o_ps"], j)
                    nc.scalar.activation(phT[:, :, :], psT[:, 0, :, 0:SUB], ACT.Copy).then_inc(S["phT"], 1)
                if there_n:
                    x_transposed(n)
                if there_i:
                    act.wait_ge(S["gT_ps"], i + 1)
                    wait(act, S["at"], i + 2 - NT)
                    for c in range(DC):
                        last = nc.scalar.activation(gate[:, it, c, :], psP[:, c, :], ACT.Tanh,
                                                    bias=bg[:, c:c + 1], scale=0.5)
                    last.then_inc(S["gate"], 1)
                    act.wait_ge(S["qkT"], i + 1)
                    wait(act, S["s_ps"], i)
                    for h in range(HC):
                        last = nc.scalar.activation(kbd[:, it % 2, 1, :, h], qkT[:, it % 2, DC + 1, :], ACT.Copy,
                                                    scale=hm[:, h:h + 1])
                    last.then_inc(S["kbd1"], 1)
                if there_w:
                    act.wait_ge(S["v_ready"], w + 1)
                    wait(act, S["o_ps"], w - 1)
                    v = KV[:, wt, D:2 * D].rearrange("p (g a d) -> p g a d", a=2, d=HD)
                    for a in range(2):
                        last = nc.scalar.activation(vp[:, wt % 2, :, a, HD * a:HD * (a + 1)], v[:, :, a, :], ACT.Copy)
                    last.then_inc(S["vp"], 1)

                if there_s:
                    waits(act, S["act_passed"], (S[f"s_stored{st % 2}"], dma_count(s, st)),
                          (S["shifted"], s))
                    act.dma_start(flat(lg[:, 0:NEAR, :]), band(s_dram[st % 2])).then_inc(S[f"near{st % 2}"], 16)

            rows(act, step)

        @block.tensor
        def _(pe):
            pe.wait_ge(S["weights"], 16 * LOADS)
            pe.wait_ge(S["scaled"], DC + 4)
            pe.wait_ge(S["zeros"], 2)

            def transpose_x(n):
                pe.wait_ge(S["xn"], n + 1)
                wait(pe, S["qkT"], n)
                for c in range(DC):
                    last = nc.tensor.transpose(psX[:, c, :], xn[:, c * P:(c + 1) * P], ident[:, :])
                last.then_inc(S["xT_ps"], 1)

            def step(T, t):
                n, nt, there_n = stage(T, t, 0)
                i, it, there_i = stage(T, t, LAG_P)
                s, st, there_s = stage(T, t, LAG_S)
                j, jt, there_j = stage(T, t, LAG_V)
                o, ot, there_o = stage(T, t, LAG_O)

                def transpose_heads(g):
                    wait(pe, S["pT"], 4 * j + g - 1)
                    if g == 0:
                        wait(pe, S["phT"], j)
                    for a in range(4):
                        last = nc.tensor.transpose(psT[:, g % 2, a, :], pd[:, SUB:KEYS, 4 * g + a], ident[:, :])
                    last.then_inc(S["pt_ps"], 1)

                def values(g):
                    pe.wait_ge(S["pT"], 4 * j + g + 1)
                    for a in range(4):
                        h = 4 * g + a
                        r = (h // 2 % 4) * 2 * HD
                        last = nc.tensor.matmul(psO[r:r + 2 * HD, g // 2, :], vp[:, jt % 2, h // 2, a % 2, :],
                                                pT[:, g % 2, a, :], start=False, stop=False, skip_group_check=True)
                    last.then_inc(S["pv_used"], 1)

                def open_chunk(c):
                    nc.tensor.matmul(psO[:, c, :], ftok[:, jt % 2, c * P:(c + 1) * P], ident[:, :],
                                     is_transpose=True, start=True, stop=False, skip_group_check=True)

                def close_chunk(c):
                    for g in (2 * c, 2 * c + 1):
                        last = nc.tensor.matmul(psO[64 * (g % 2):64 * (g % 2) + 64, c, 0:SUB],
                                                flat(vh[:, jt % 2, g, :, :]), phT[:, g, :],
                                                start=False, stop=True, skip_group_check=True)
                    return last

                if there_i:
                    pe.wait_ge(S["xT"], i + 1)
                    wait(pe, S["gate"], i)
                    wait(pe, S["gtok"], i)
                    for c in range(DC):
                        nc.tensor.matmul(psP[:, :, :], xT[:, c, :], wqkv[:, c, 0:2 * D],
                                         start=(c == 0), stop=(c == DC - 1))
                    for dst, w in ((psG[:, 0:DC, :], wqkv[:, :, 2 * D:3 * D]), (psG[:, DC:4, :], wg[:, :, :])):
                        for c in range(DC):
                            last = nc.tensor.matmul(flat(dst), xT[:, c, :], w[:, c, :],
                                                    start=(c == 0), stop=(c == DC - 1))
                    last.then_inc(S["pr_ps"], 1)
                if there_o:
                    pe.wait_ge(S["at"], o + 1)
                    for c in range(DC):
                        last = nc.tensor.matmul(flat(psO[:, DC:4, :]), at[:, c, :], wo[:, c, :],
                                                start=(c == 0), stop=(c == DC - 1))
                    last.then_inc(S["out_ps"], 1)
                if there_i:
                    pe.wait_ge(S["q_tok"], i + 1)
                    pe.wait_ge(S["k_ready"], i + 1)
                    pe.wait_ge(S["xT"], i + 1)
                    for c in range(DC):
                        nc.tensor.transpose(psX[:, c, :], qtok[:, it % 2, c * P:(c + 1) * P], ident[:, :])
                    for c in range(DC):
                        last = nc.tensor.transpose(psX[:, DC + c, :], KV[:, it, c * P:(c + 1) * P], ident[:, :])
                    last.then_inc(S["qkT_ps"], 1)
                if there_s:
                    wait(pe, S["ssb"], s)
                    for c in range(DC):
                        last = nc.tensor.matmul(psS[:, c, 0:NO * HC], qkT[:, st % 2, c, :], se[:, :],
                                                start=True, stop=True)
                    last.then_inc(S["qs_ps"], 1)
                if there_j:
                    pe.wait_ge(S[f"band{jt % 2}"], dma_count(j, jt, NSUB))
                    transpose_heads(0)
                    transpose_heads(1)
                if there_i:
                    pe.wait_ge(S["gtok"], i + 1)
                    for c in range(DC):
                        last = nc.tensor.transpose(psP[:, c, :], gtok[:, c * P:(c + 1) * P], ident[:, :])
                    last.then_inc(S["gT_ps"], 1)
                if there_s:
                    pe.wait_ge(S["kbd0"], s + 1)
                    pe.wait_ge(S["kbd1"], s + 1)
                    pe.wait_ge(S["qs1"], s + 1)
                    for c in range(DC):
                        for b in range(NSUB):
                            r = slice(SUB * b, SUB * (b + 1))
                            q = qkT[:, st % 2, c, r]
                            if b == 0:
                                nc.tensor.matmul(psS[r, c, 0:SUB * HC], q, flat(kbd[:, 1 - st % 2, c, P - SUB:P, :]),
                                                 start=True, stop=True)
                                last = nc.tensor.matmul(psS[r, c, SUB * HC:WIN * HC], q,
                                                        flat(kbd[:, st % 2, c, 0:SUB, :]), start=True, stop=True)
                            else:
                                k0 = SUB * (b - 1)
                                last = nc.tensor.matmul(psS[r, c, :], q, flat(kbd[:, st % 2, c, k0:k0 + WIN, :]),
                                                        start=True, stop=True)
                    last.then_inc(S["s_ps"], 1)
                if there_j:
                    pe.wait_ge(S["ftok"], j + 1)
                    pe.wait_ge(S["vp"], j + 1)
                    pe.wait_ge(S["vh"], (j + 1) * 64)
                    wait(pe, S["with_out"], j)
                    open_chunk(0)
                    values(0)
                    transpose_heads(2)
                    values(1)
                    transpose_heads(3)
                    waits(pe, S["passed"], (S["pT"], 4 * j + 3), (S["ph"], j + 1))
                    for g in range(4):
                        last = nc.tensor.transpose(psT[:, 0, g, 0:SUB],
                                                   ph[:, 4 * g:4 * g + 4, :].rearrange("p h k -> p (h k)"),
                                                   ident[0:SUB, 0:SUB])
                    last.then_inc(S["pt_halo_ps"], 1)
                if there_n:
                    transpose_x(n)
                if there_j:
                    pe.wait_ge(S["phT"], j + 1)
                    close_chunk(0)
                    open_chunk(1)
                    values(2)
                    values(3)
                    close_chunk(1).then_inc(S["o_ps"], 1)

            rows(pe, step)


def macaron(nc, x, x_out, s_dram, p_dram, c):
    with ExitStack() as ctx:
        X = ctx.enter_context(nc.sbuf_tensor("X", [P, TILES, D], F32))
        mean_all = ctx.enter_context(nc.sbuf_tensor("mean_all", [P, TILES], F32))
        rstd_all = ctx.enter_context(nc.sbuf_tensor("rstd_all", [P, TILES], F32))
        ffn = (c["w_r"], c["w_k"], c["w_v"], c["mu_r"], c["mu_k"], c["ident"])
        ffn_phase(nc, X, x, None, *ffn, "f0_", (mean_all, rstd_all))
        attention_phase(nc, X, mean_all, rstd_all, c["w_qkv"], c["w_gate"], c["w_out"], c["qkv_bias"],
                        c["gate_bias"], c["out_bias"], c["gain"], c["scale_rows"], c["pos_rows"], c["masks"],
                        c["ident"], c["head_mask"], s_dram, p_dram)
        ffn_phase(nc, X, None, x_out, *ffn, "f1_", None)


def kernel(**inputs):
    import numpy as np
    import concourse.bacc as bacc
    from concourse.bass_utils import run_bass_kernel_spmd

    a = {k.replace("L0_", ""): np.asarray(v) for k, v in inputs.items()}
    f32 = np.float32
    order = list(range(NEAR - 1, -1, -1)) + list(range(NEAR, NO))

    def columns(v):
        return v.reshape(-1, P).T

    scale_rows = np.zeros((HC, HD, NO, HC), f32)
    for h in range(HC):
        scale_rows[h, :, :, h] = a["attn_scale_embed"][order].T
    offsets = np.array(list(range(NEAR - 1, -1, -1)) + FAR)
    masks = np.zeros((P, MASKED, NO), f32)
    for t in range(MASKED):
        masks[:, t, :] = np.where(np.arange(P)[:, None] + P * t >= offsets[None, :], 0.0, -1e30)
    row = np.arange(P)
    arrays = {
        "x": a["attn_x"].reshape(B * N, D),
        "w_r": a["ffn_W_r"].T, "w_k": a["ffn_W_k"].T, "w_v": a["ffn_W_v"].T,
        "mu_r": columns(a["ffn_mu_r"]), "mu_k": columns(a["ffn_mu_k"]),
        "w_qkv": a["attn_qkv_w"].T, "w_gate": a["attn_gate_w"].T, "w_out": a["attn_out_w"].T,
        "qkv_bias": a["attn_qkv_b"],
        "gate_bias": columns(a["attn_gate_b"]), "out_bias": a["attn_out_b"],
        "gain": columns(np.repeat(a["attn_if_gain"], HD)),
        "scale_rows": scale_rows.reshape(P, NO * HC), "pos_rows": a["attn_pos_bias"][order].reshape(-1),
        "masks": masks, "ident": np.eye(P, dtype=f32),
        "head_mask": (row[:, None] // HD == np.arange(HC)[None, :]).astype(f32),
    }
    arrays = {k: np.ascontiguousarray(v) for k, v in arrays.items()}
    nc = bacc.Bacc("TRN2", target_bir_lowering=False, num_devices=1)
    aps = {k: nc.dram_tensor(k, list(v.shape), F32, kind="ExternalInput").ap() for k, v in arrays.items()}
    out = nc.dram_tensor("out", [B * N, D], F32, kind="ExternalOutput").ap()
    s_dram = [nc.dram_tensor(f"s_scratch{i}", [P * WIN * H], F32, kind="Internal").ap() for i in range(2)]
    p_dram = [nc.dram_tensor(f"p_scratch{i}", [P * WIN * H], F32, kind="Internal").ap() for i in range(2)]
    x = aps.pop("x")
    macaron(nc, x, out, s_dram, p_dram, aps)
    r = run_bass_kernel_spmd(nc, [arrays], core_ids=[0])
    return r.results[0]["out"].reshape(B, N, D)
```

```python
import concourse.bass as bass
from concourse import mybir
from contextlib import ExitStack

F32 = mybir.dt.float32
F32R = mybir.dt.float32r
ALU = mybir.AluOpType
ACT = mybir.ActivationFunctionType
AX = mybir.AxisListType

P = 128
B, N, D, H = 8, 1024, 256, 16
HD = D // H
DC = D // P
HC = H // DC
NT = N // P
TILES = B * NT
EPS = 1e-5

NEAR = 33
SUB = 32
WIN = 2 * SUB
NSUB = P // SUB
FAR = [48, 96, 192, 64, 384, 256, 128]
NO = NEAR + len(FAR)
NF = len(FAR)
LOC = NEAR * H
ALL = NO * H
MASKED = max(FAR) // P
GROUP = 4
NG = TILES // GROUP
LAG_P, LAG_S, LAG_M, LAG_F, LAG_W, LAG_V, LAG_O = 1, 2, 3, 4, 4, 5, 6


def wait(eng, sem, value):
    if isinstance(value, int) and value <= 0:
        return
    eng.wait_ge(sem, value)


def waits(eng, passed, *pairs):
    for sem, value in pairs:
        if isinstance(value, int) and value <= 0:
            continue
        eng.wait_ge(sem, value).then_inc(passed, 1)


def ffn_phase(nc, X, x_in, out, w_r, w_k, w_v, mu_r, mu_k, ident, s_ident, tag, stats_after, preload):
    ctx = ExitStack()
    with ctx:
        def sb(name, shape, dtype=F32):
            return ctx.enter_context(nc.sbuf_tensor(tag + name, shape, dtype))

        def pb(name, shape):
            return ctx.enter_context(nc.psum_tensor(tag + name, shape, F32))

        def sem(name):
            return ctx.enter_context(nc.semaphore(tag + name))

        GT = GROUP * P
        wr = sb("wr", [P, DC, D])
        wk = sb("wk", [P, DC, D])
        wv = sb("wv", [P, DC, D])
        mur = sb("mur", [P, DC])
        muk = sb("muk", [P, DC])
        mhalf = sb("mhalf", [P, GROUP])
        st = sb("st", [P, 2, GROUP, 6])
        mv = sb("mv", [P, 2, GROUP, 2])
        ve = sb("ve", [P, 2, GROUP])
        rstd = sb("rstd", [P, 2, GROUP])
        xn = sb("xn", [P, 2, GROUP, D])
        xT = sb("xT", [P, 2, DC, 1 + GT])
        dx = sb("dx", [P, 2, DC, GT])
        xr = sb("xr", [P, 2, DC, GT])
        xk = sb("xk", [P, 2, DC, GT])
        xkh = sb("xkh", [P, 2, DC, GT], F32R)
        xkl = sb("xkl", [P, 2, DC, GT], F32R)
        wkh = sb("wkh", [P, DC, D], F32R)
        wkl = sb("wkl", [P, DC, D], F32R)
        kr = sb("kr", [P, DC, GT])
        ka = sb("ka", [P, 2, DC, GT])
        th = sb("th", [P, 2, GROUP, D])
        rv = sb("rv", [P, 2, GROUP, D])
        st2 = sb("st2", [P, 2, GROUP, 6])
        mv2 = sb("mv2", [P, 2, GROUP, 2])
        ve2 = sb("ve2", [P, 2, GROUP])
        nm2 = sb("nm2", [P, 2, GROUP])

        psT = pb("psT", [P, DC, GT])
        psK = pb("psK", [P, DC, GT])
        psR = pb("psR", [P, GROUP, D])
        psV = pb("psV", [P, GROUP, D])

        s_mu = sem("mu_loaded")
        s_wk = sem("wk_loaded")
        s_wrv = sem("wr_wv_loaded")
        s_x = sem("x_loaded")
        s_c = sem("constants_set")
        s_st = sem("stats_of_tile")
        s_mv = sem("mean_var_of_tile")
        s_ve = sem("var_plus_eps")
        s_rs = sem("rstd_ready")
        s_xn = sem("xn_ready")
        s_T = sem("transposed_in_psum")
        s_xT = sem("xT_ready")
        s_dx = sem("dx_ready")
        s_mix = sem("mixed_ready")
        s_wh = sem("wk_high_part")
        s_wl = sem("wk_low_part")
        s_hi = sem("xk_high_part")
        s_lo = sem("xk_low_part")
        s_K = sem("k_in_psum")
        s_kr = sem("relu_done")
        s_ka = sem("squared_ready")
        s_R = sem("r_in_psum")
        s_th = sem("tanh_ready")
        s_V = sem("v_in_psum")
        s_rv = sem("rv_done")
        s_res = sem("residual_done")
        s_st2 = sem("new_stats")
        s_mv2 = sem("new_mean_var")
        s_ve2 = sem("new_var_plus_eps")
        s_rs2 = sem("new_rstd")
        s_out = sem("stored")
        s_passed = sem("waits_passed")

        block = ctx.enter_context(nc.Block())
        GB = NT // GROUP

        @block.sync
        def _(sp):
            def load_x(g):
                wait(sp, s_x, 16 * g)
                sp.dma_start(X[:, g * GROUP:(g + 1) * GROUP, :],
                             x_in.rearrange("(t p) d -> p t d", p=P)[:, g * GROUP:(g + 1) * GROUP, :]).then_inc(s_x, 16)

            if x_in is not None:
                load_x(0)
            for dst, src, loaded in ((muk[:, :], mu_k, s_mu), (mur[:, :], mu_r, s_mu),
                                     (wk[:, :, :], w_k.rearrange("(c p) n -> p c n", p=P), s_wk),
                                     (wr[:, :, :], w_r.rearrange("(c p) n -> p c n", p=P), s_wrv),
                                     (wv[:, :, :], w_v.rearrange("(c p) n -> p c n", p=P), s_wrv)):
                sp.dma_start(dst, src).then_inc(loaded, 16)
            if x_in is not None:
                for g in range(1, NG):
                    load_x(g)
            if preload is not None:
                preload(sp)
            if out is not None:
                ov = out.rearrange("(t p) d -> p t d", p=P)
                for g in range(NG):
                    sp.wait_ge(s_res, g + 1)
                    sp.dma_start(ov[:, g * GROUP:(g + 1) * GROUP, :],
                                 X[:, g * GROUP:(g + 1) * GROUP, :]).then_inc(s_out, 16)
                sp.wait_ge(s_out, 16 * NG)

        @block.vector
        def _(dve):
            nc.vector.memset(mhalf[:, :], -0.5).then_inc(s_c, 1)
            nc.vector.memset(xT[:, 0, :, 0:1], 0.0).then_inc(s_c, 1)

            def stats(G, par):
                if x_in is not None:
                    waits(dve, s_passed, (s_x, 16 * (G + 1)))
                for u in range(GROUP):
                    nc.vector.bn_stats(st[:, par, u, :], X[:, G * GROUP + u, :]).then_inc(s_st, 1)
                for u in range(GROUP):
                    waits(dve, s_passed, (s_st, GROUP * G + u + 1))
                    nc.vector.bn_aggr(mv[:, par, u, :], st[:, par, u, :]).then_inc(s_mv, 1)
                dve.wait_ge(s_mv, GROUP * (G + 1))
                nc.vector.tensor_scalar(ve[:, par, :], mv[:, par, :, 1], EPS, None, ALU.add).then_inc(s_ve, 1)

            def norm(G, par):
                dve.wait_ge(s_rs, G + 1)
                wait(dve, s_T, G - 1)
                for u in range(GROUP):
                    last = nc.vector.tensor_scalar(xn[:, par, u, :], X[:, G * GROUP + u, :],
                                                   mv[:, par, u, 0:1], rstd[:, par, u:u + 1],
                                                   ALU.subtract, ALU.mult)
                last.then_inc(s_xn, 1)

            def mix(G, par):
                dve.wait_ge(s_dx, G + 1)
                wait(dve, s_V, G - 1)
                for dst, mu in ((xk, muk), (xr, mur)):
                    for c in range(DC):
                        nc.vector.scalar_tensor_tensor(dst[:, par, c, :], dx[:, par, c, :], mu[:, c:c + 1],
                                                       xT[:, par, c, 0:GT], ALU.mult, ALU.add).then_inc(s_mix, 1)

            def final(G, par):
                dve.wait_ge(s_th, G + 1)
                dve.wait_ge(s_V, G + 1)
                nc.vector.scalar_tensor_tensor(rv[:, par, :, :], th[:, par, :, :], 1.0, psV[:, :, :],
                                               ALU.add, ALU.mult).then_inc(s_rv, 1)
                dve.wait_ge(s_rv, G + 1)
                x = X[:, bass.ds(G * GROUP, GROUP), :]
                nc.vector.scalar_tensor_tensor(x, rv[:, par, :, :], 0.25, x, ALU.mult, ALU.add).then_inc(s_res, 1)

            def new_stats(G, par):
                if stats_after is None:
                    return
                waits(dve, s_passed, (s_res, G + 1))
                for u in range(GROUP):
                    nc.vector.bn_stats(st2[:, par, u, :], X[:, G * GROUP + u, :]).then_inc(s_st2, 1)
                waits(dve, s_passed, (s_rs2, 2 * (G - 1)))
                for u in range(GROUP):
                    waits(dve, s_passed, (s_st2, GROUP * G + u + 1))
                    nc.vector.bn_aggr(mv2[:, par, u, :], st2[:, par, u, :]).then_inc(s_mv2, 1)
                dve.wait_ge(s_mv2, GROUP * (G + 1))
                nc.vector.tensor_scalar(nm2[:, par, :], mv2[:, par, :, 0], -1.0, None, ALU.mult).then_inc(s_ve2, 1)
                nc.vector.tensor_scalar(ve2[:, par, :], mv2[:, par, :, 1], EPS, None, ALU.add).then_inc(s_ve2, 1)

            dve.wait_ge(s_c, 2)
            stats(0, 0)
            norm(0, 0)
            stats(1, 1)
            norm(1, 1)
            dve.wait_ge(s_mu, 32)
            mix(0, 0)

            def ahead(G, g, first=False):
                stats(G + 2, g)
                mix(G + 1, 1 - g)
                norm(G + 2, g)
                if not first:
                    new_stats(G - 1, 1 - g)
                final(G, g)

            for g in range(GB):
                ahead(g, g, g == 0)
            with dve.Fori(1, B - 1) as b:
                for g in range(GB):
                    ahead(b * GB + g, g)
            mix(NG - 1, 1)
            new_stats(NG - 3, 1)
            final(NG - 2, 0)
            new_stats(NG - 2, 0)
            final(NG - 1, 1)
            new_stats(NG - 1, 1)

        @block.gpsimd
        def _(pool):
            pool.wait_ge(s_c, 2)

            def rs(G, par):
                pool.wait_ge(s_ve, G + 1)
                wait(pool, s_xn, G - 1)
                nc.gpsimd.tensor_tensor(rstd[:, par, :], ve[:, par, :], mhalf[:, :], ALU.pow).then_inc(s_rs, 1)

            def low(G, par):
                pool.wait_ge(s_hi, G + 1)
                wait(pool, s_K, G - 1)
                nc.gpsimd.tensor_tensor(xkl[:, par, :, :], xk[:, par, :, :], xkh[:, par, :, :].bitcast(F32),
                                        ALU.subtract).then_inc(s_lo, 1)

            def diff(G, par):
                pool.wait_ge(s_xT, G + 1)
                wait(pool, s_mix, 2 * DC * (G - 1))
                nc.gpsimd.tensor_tensor(dx[:, par, :, :], xT[:, par, :, 1:1 + GT], xT[:, par, :, 0:GT],
                                        ALU.subtract).then_inc(s_dx, 1)

            def new(G, par):
                if stats_after is None:
                    return
                shift_all, rstd_all = stats_after
                now = bass.ds(G * GROUP, GROUP)
                pool.wait_ge(s_ve2, 2 * (G + 1))
                nc.gpsimd.tensor_tensor(rstd_all[:, now], ve2[:, par, :], mhalf[:, :], ALU.pow).then_inc(s_rs2, 1)
                pool.wait_ge(s_rs2, 2 * G + 1)
                nc.gpsimd.tensor_tensor(shift_all[:, now], nm2[:, par, :], rstd_all[:, now], ALU.mult)\
                    .then_inc(s_rs2, 1)

            rs(0, 0)
            rs(1, 1)
            diff(0, 0)
            pool.wait_ge(s_wh, 1)
            nc.gpsimd.tensor_tensor(wkl[:, :, :], wk[:, :, :], wkh[:, :, :].bitcast(F32), ALU.subtract).then_inc(s_wl, 1)
            low(0, 0)

            def ahead(G, g, first=False):
                diff(G + 1, 1 - g)
                rs(G + 2, g)
                low(G + 1, 1 - g)
                if not first:
                    new(G - 1, 1 - g)

            for g in range(GB):
                ahead(g, g, g == 0)
            with pool.Fori(1, B - 1) as b:
                for g in range(GB):
                    ahead(b * GB + g, g)
            diff(NG - 1, 1)
            low(NG - 1, 1)
            new(NG - 3, 1)
            new(NG - 2, 0)
            new(NG - 1, 1)

        @block.scalar
        def _(act):
            def xt(G, par):
                act.wait_ge(s_T, G + 1)
                wait(act, s_mix, 2 * DC * (G - 1))
                last = nc.scalar.activation(xT[:, par, :, 1:1 + GT], psT[:, :, :], ACT.Copy)
                if par:
                    act.wait_ge(s_xT, G)
                    last = nc.scalar.activation(xT[:, 1, :, 0:1], xT[:, 0, :, GT:GT + 1], ACT.Copy)
                last.then_inc(s_xT, 1)

            def high(G, par):
                act.wait_ge(s_mix, 2 * DC * G + DC)
                wait(act, s_K, G - 1)
                nc.scalar.activation(xkh[:, par, :, :], xk[:, par, :, :], ACT.Copy).then_inc(s_hi, 1)

            def rest(G, par, more=True):
                act.wait_ge(s_K, G + 1)
                wait(act, s_ka, G)
                nc.scalar.activation(kr[:, :, :], psK[:, :, :], ACT.Relu).then_inc(s_kr, 1)
                act.wait_ge(s_kr, G + 1)
                wait(act, s_V, G - 1)
                nc.scalar.activation(ka[:, par, :, :], kr[:, :, :], ACT.Square).then_inc(s_ka, 1)
                if more:
                    high(G + 1, 1 - par)
                act.wait_ge(s_R, G + 1)
                wait(act, s_rv, G - 1)
                nc.scalar.activation(th[:, par, :, :], psR[:, :, :], ACT.Tanh, scale=0.5).then_inc(s_th, 1)

            act.wait_ge(s_wk, 16)
            nc.scalar.activation(wkh[:, :, :], wk[:, :, :], ACT.Copy).then_inc(s_wh, 1)
            xt(0, 0)
            high(0, 0)

            def ahead(G, g):
                xt(G + 1, 1 - g)
                rest(G, g)

            for g in range(GB):
                ahead(g, g)
            with act.Fori(1, B - 1) as b:
                for g in range(GB):
                    ahead(b * GB + g, g)
            xt(NG - 1, 1)
            rest(NG - 2, 0)
            rest(NG - 1, 1, more=False)

        @block.tensor
        def _(pe):
            def tr(G, par):
                pe.wait_ge(s_xn, G + 1)
                wait(pe, s_xT, G)
                for c in range(DC):
                    for u in range(GROUP):
                        last = nc.tensor.transpose(psT[:, c, u * P:(u + 1) * P], xn[:, par, u, c * P:(c + 1) * P],
                                                   ident[:, :])
                last.then_inc(s_T, 1)

            def products(G, par):
                pe.wait_ge(s_lo, G + 1)
                wait(pe, s_kr, G)
                parts = [(w, x, c) for c in range(DC) for w, x in ((wkh, xkh), (wkh, xkl), (wkl, xkh))]
                for e in range(DC):
                    for w, x, c in parts:
                        last = nc.tensor.matmul(psK[:, e, :], w[:, c, e * P:(e + 1) * P], x[:, par, c, :],
                                                start=(w is wkh and x is xkh and c == 0),
                                                stop=(w is wkl and c == DC - 1))
                last.then_inc(s_K, 1)
                pe.wait_ge(s_mix, 2 * DC * (G + 1))
                wait(pe, s_th, G)
                for u in range(GROUP):
                    for c in range(DC):
                        last = nc.tensor.matmul(psR[:, u, :], xr[:, par, c, u * P:(u + 1) * P], wr[:, c, :],
                                                start=(c == 0), stop=(c == DC - 1))
                last.then_inc(s_R, 1)
                pe.wait_ge(s_ka, G + 1)
                wait(pe, s_rv, G)
                for u in range(GROUP):
                    for c in range(DC):
                        last = nc.tensor.matmul(psV[:, u, :], ka[:, par, c, u * P:(u + 1) * P], wv[:, c, :],
                                                start=(c == 0), stop=(c == DC - 1))
                last.then_inc(s_V, 1)

            pe.wait_ge(s_ident, 16)
            tr(0, 0)
            pe.wait_ge(s_wl, 1)
            pe.wait_ge(s_wrv, 32)

            def ahead(G, g):
                tr(G + 1, 1 - g)
                products(G, g)

            for g in range(GB):
                ahead(g, g)
            with pe.Fori(1, B - 1) as b:
                for g in range(GB):
                    ahead(b * GB + g, g)
            tr(NG - 1, 1)
            products(NG - 2, 0)
            products(NG - 1, 1)


class AttentionConstants:

    def __init__(self, nc, ctx, c):
        def sb(name, shape):
            return ctx.enter_context(nc.sbuf_tensor("a_" + name, shape, F32))

        self.wqkv = sb("wqkv", [P, DC, 3 * D])
        self.wg = sb("wg", [P, DC, D])
        self.wo = sb("wo", [P, DC, D])
        self.bqkv = sb("bqkv", [P, 3 * D])
        self.bg = sb("bg", [P, DC])
        self.ob = sb("ob", [P, D])
        self.gn = sb("gn", [P, DC])
        self.se = sb("se", [P, NO * HC])
        self.hm = sb("hm", [P, HC])
        self.bias = sb("bias", [P, ALL])
        self.mask = sb("mask", [P, MASKED, NO])
        self.loads = [
            (self.wqkv[:, :, :], c["w_qkv"].rearrange("(c p) n -> p c n", p=P)),
            (self.wg[:, :, :], c["w_gate"].rearrange("(c p) n -> p c n", p=P)),
            (self.wo[:, :, :], c["w_out"].rearrange("(c p) n -> p c n", p=P)),
            (self.bqkv[:, :], c["qkv_bias"].partition_broadcast(P)), (self.bg[:, :], c["gate_bias"]),
            (self.gn[:, :], c["gain"]), (self.ob[:, :], c["out_bias"].partition_broadcast(P)),
            (self.se[:, :], c["scale_rows"]), (self.hm[:, :], c["head_mask"]),
            (self.bias[:, :], c["pos_rows"].partition_broadcast(P)), (self.mask[:, :, :], c["masks"])]
        self.loaded = ctx.enter_context(nc.semaphore("a_constants_loaded"))
        self.full = 16 * len(self.loads)

    def load(self, sp):
        for dst, src in self.loads:
            sp.dma_start(dst, src).then_inc(self.loaded, 16)


def attention_phase(nc, X, shift_all, rstd_all, consts, ident, s_dram, p_dram):
    ctx = ExitStack()
    with ctx:
        def sb(name, shape):
            return ctx.enter_context(nc.sbuf_tensor("a_" + name, shape, F32))

        def pb(name, shape):
            return ctx.enter_context(nc.psum_tensor("a_" + name, shape, F32))

        def sem(name):
            return ctx.enter_context(nc.semaphore("a_" + name))

        KEYS = SUB + P
        wqkv, wg, wo, bqkv, bg, ob = consts.wqkv, consts.wg, consts.wo, consts.bqkv, consts.bg, consts.ob
        gn, se, hm, bias, mask = consts.gn, consts.se, consts.hm, consts.bias, consts.mask
        xn = sb("xn", [P, D])
        xT = sb("xT", [P, DC, P])
        qkT = sb("qkT", [P, 2, 2 * DC, P])
        kbd = sb("kbd", [P, 2, DC, P, HC])
        gtok = sb("gtok", [P, D])
        gate = sb("gate", [P, NT, DC, P])
        qtok = sb("qtok", [P, 2, D])
        KV = sb("KV", [P, NT, 2 * D])
        S64 = sb("S64", [P, 8, 1, D])
        S4896 = sb("S4896", [P, 6, 2, D])
        vp = sb("vp", [P, 2, H // 2, 2, 2 * HD])
        vh = sb("vh", [P, 2, H // 4, 4, HD])
        ssb = sb("ssb", [P, WIN, H])
        qs1 = sb("qs1", [P, NO, H])
        lg = sb("lg", [P, NO, H])
        ex = sb("ex", [P, 2, NO, H])
        mx = sb("mx", [P, H])
        sm = sb("sm", [P, H])
        rs = sb("rs", [P, H])
        fqk = sb("fqk", [P, NF, D])
        fpv = sb("fpv", [P, NF, D])
        ftok = sb("ftok", [P, 2, D])
        pd = sb("pd", [P, KEYS, H])
        ph = sb("ph", [SUB, H, SUB])
        pT = sb("pT", [P, 2, 4, P])
        phT = sb("phT", [P, 4, SUB])
        at = sb("at", [P, DC, P])

        psX = pb("psX", [P, 4, P])
        psP = pb("psP", [P, 4, P])
        psG = pb("psG", [P, 4, P])
        psS = pb("psS", [P, DC, 512])
        psT = pb("psT", [P, 2, 4, P])
        psO = pb("psO", [P, 4, P])

        names = """scaled zeros xn xT_ps xT qk_ps pr_ps q_tok k_ready v_ready gtok qkT_ps qkT gT_ps gate
            moved0 moved1 vp vh kbd0 kbd1 qs_ps qs1 s_ps ssb s_stored0 s_stored1 near0 near1
            fqk far_lg prod biased masked mx shifted ex sm rs p_ready fpv ftok p_stored0 p_stored1 band0 band1
            pt_ps pt_halo_ps ph pv_used pT phT o_ps at out_ps with_out x_new passed sp_passed""".split()
        S = {n: sem(n) for n in names}
        block = ctx.enter_context(nc.Block())

        def rows(eng, step):
            for t in range(NT):
                step(t, t)
            with eng.Fori(1, B) as b:
                for t in range(NT):
                    step(b * NT + t, t)
            for t in range(LAG_O):
                step(TILES + t, t)

        def stage(T, t, lag):
            return T - lag, (t - lag) % NT, not isinstance(T, int) or 0 <= T - lag < TILES

        def dma_count(T, t, per=1):
            return 16 * per * (T // 2 + 1) if isinstance(T, int) else (T - t) * (8 * per) + 16 * per * (t // 2 + 1)

        SHIFTED = ((48, S4896, 0, 2), (64, S64, 0, 4), (96, S4896, 1, 2))
        ROW = WIN * H

        def band(dram):
            return bass.AP(dram.tensor, dram.offset, [[SUB * ROW, NSUB], [ROW + H, SUB], [1, LOC]])

        def by_rows(dram):
            return dram.rearrange("(p k) -> p k", p=P)

        def flat(a):
            return a.rearrange("p a b -> p (a b)")

        @block.sync
        def _(sp):
            sp.wait_ge(S["zeros"], 1)
            for par in range(2):
                sp.dma_start(by_rows(p_dram[par]), flat(pd[:, 0:WIN, :])).then_inc(S[f"p_stored{par}"], 16)
            sp.wait_ge(S["zeros"], 2)

            def step(T, t):
                s, st, there_s = stage(T, t, LAG_S)
                if there_s:
                    waits(sp, S["sp_passed"], (S["ssb"], s + 1), (S[f"near{st % 2}"], dma_count(s, st) - 16))
                    sp.dma_start(by_rows(s_dram[st % 2]), flat(ssb[:, :, :])).then_inc(S[f"s_stored{st % 2}"], 16)
                i, it, there = stage(T, t, LAG_P)
                if there:
                    waits(sp, S["sp_passed"], (S["k_ready"], i + 1), (S["v_ready"], i + 1),
                          (S["fqk"], i - 1), (S["fpv"], i - 2))
                    for sh, buf, place, ks in SHIFTED:
                        k, v = it % ks, ks + it % 4
                        for dst, src in ((buf[0:sh], KV[P - sh:P, (it - 1) % NT, :]), (buf[sh:P], KV[0:P - sh, it, :])):
                            sp.dma_start(dst[:, k:v + 1:v - k, place, :], src.rearrange("p (a d) -> p a d", a=2))\
                                .then_inc(S[f"moved{it % 2}"], 16)
                if there_s:
                    waits(sp, S["sp_passed"], (S[f"s_stored{st % 2}"], dma_count(s, st)), (S["shifted"], s))
                    sp.dma_start(flat(lg[:, 0:NEAR, :]), band(s_dram[st % 2])).then_inc(S[f"near{st % 2}"], 16)
                m, mt, there = stage(T, t, LAG_M)
                if there:
                    mp = mt % 2
                    waits(sp, S["sp_passed"], (S["p_ready"], m + 1),
                          (S[f"band{mp}"], dma_count(m, mt, NSUB) - 16 * NSUB), (S[f"p_stored{mp}"], dma_count(m, mt)))
                    sp.dma_start(band(p_dram[mp]), flat(ex[:, mp, 0:NEAR, :])).then_inc(S[f"p_stored{mp}"], 16)
                w, wt, there_w = stage(T, t, LAG_W)
                if there_w:
                    waits(sp, S["sp_passed"], (S["pt_ps"], 4 * w), (S["ph"], w),
                          (S[f"p_stored{wt % 2}"], dma_count(w, wt) + 16))
                    for b in range(NSUB):
                        sp.dma_start(flat(pd[SUB * b:SUB * (b + 1), SUB * b:SUB * b + WIN, :]),
                                     by_rows(p_dram[wt % 2])[SUB * b:SUB * (b + 1), :]).then_inc(S[f"band{wt % 2}"], 16)
                    waits(sp, S["sp_passed"], (S["o_ps"], w))
                    for j in range(4):
                        sp.dma_start(vh[SUB * j:SUB * (j + 1), wt % 2, :, j, :],
                                     KV[P - SUB:P, (wt - 1) % NT, D:2 * D]
                                     .rearrange("p (g a d) -> p g a d", a=4, d=HD)[:, :, j, :]).then_inc(S["vh"], 16)

            rows(sp, step)

        @block.vector
        def _(dve):
            dve.wait_ge(consts.loaded, consts.full)
            scale = HD ** -0.5
            for c in range(DC):
                nc.vector.tensor_scalar(wo[:, c, :], wo[:, c, :], gn[:, c:c + 1], 0.5, ALU.mult, ALU.mult)\
                    .then_inc(S["scaled"], 1)
            for a, by in ((bg[:, :], 0.5), (wqkv[:, :, 0:D], scale), (bqkv[:, 0:D], scale), (se[:, :], 1 / scale)):
                nc.vector.tensor_scalar(a, a, by, None, ALU.mult).then_inc(S["scaled"], 1)
            dve.wait_ge(S["scaled"], DC + 4)

            def step(T, t):
                i, it, there_i = stage(T, t, LAG_P)
                m, mt, there_m = stage(T, t, LAG_M)
                mp = mt % 2
                f, ft, there_f = stage(T, t, LAG_F)
                o, ot, there_o = stage(T, t, LAG_O)
                if there_m:
                    dve.wait_ge(S["fqk"], m + 1)
                    nc.vector.tensor_reduce(lg[:, NEAR:NO, :], fqk[:, :, :].rearrange("p o (h d) -> p (o h) d", d=HD),
                                            AX.X, ALU.add).then_inc(S["far_lg"], 1)
                if there_o:
                    dve.wait_ge(S["o_ps"], o + 1)
                    wait(dve, S["out_ps"], o)
                    nc.vector.scalar_tensor_tensor(at[:, :, :], gate[:, ot, :, :], 1.0, psO[:, 0:DC, :],
                                                   ALU.add, ALU.mult).then_inc(S["at"], 1)
                if there_i:
                    if isinstance(i, int) and i == 1:
                        dve.wait_ge(S["zeros"], 2)
                    dve.wait_ge(S["qk_ps"], i + 1)
                    wait(dve, S["fqk"], i - 1)
                    wait(dve, S["qkT_ps"], i - 1)
                    nc.vector.tensor_tensor(qtok[:, it % 2, :], flat(psP[:, 0:DC, :]), bqkv[:, 0:D], ALU.add)\
                        .then_inc(S["q_tok"], 1)
                    wait(dve, S["fpv"], i + 1 - NT + 3)
                    wait(dve, S["vh"], 64 * (i + 1 - NT + 1) if isinstance(i, int) else (i - NT + 2) * 64)
                    nc.vector.tensor_tensor(KV[:, it, 0:D], flat(psP[:, DC:4, :]), bqkv[:, D:2 * D], ALU.add)\
                        .then_inc(S["k_ready"], 1)
                    dve.wait_ge(S["pr_ps"], i + 1)
                    nc.vector.tensor_tensor(KV[:, it, D:2 * D], flat(psG[:, 0:DC, :]), bqkv[:, 2 * D:3 * D], ALU.add)\
                        .then_inc(S["v_ready"], 1)
                if there_m:
                    dve.wait_ge(S["far_lg"], m + 1)
                    dve.wait_ge(S["qs1"], m + 1)
                    dve.wait_ge(S[f"near{mp}"], dma_count(m, mt))
                    nc.vector.tensor_tensor(flat(lg[:, :, :]), flat(lg[:, :, :]), flat(qs1[:, :, :]), ALU.mult)\
                        .then_inc(S["prod"], 1)
                    dve.wait_ge(S["prod"], m + 1)
                    nc.vector.tensor_tensor(flat(lg[:, :, :]), flat(lg[:, :, :]), bias[:, :],
                                            ALU.add).then_inc(S["biased"], 1)
                    dve.wait_ge(S["biased"], m + 1)
                    if mt < MASKED:
                        o0 = 0 if mt == 0 else NEAR
                        rest = 1 if mt < MASKED - 1 else NT + 1 - MASKED
                        nc.vector.tensor_tensor(lg[:, o0:NO, :], lg[:, o0:NO, :],
                                                mask[:, mt, o0:NO].unsqueeze(2).to_broadcast([P, NO - o0, H]),
                                                ALU.add).then_inc(S["masked"], rest)
                        dve.wait_ge(S["masked"], m + rest)
                    nc.vector.tensor_reduce(mx[:, :], lg[:, :, :].rearrange("p o h -> p h o"),
                                            AX.X, ALU.max).then_inc(S["mx"], 1)
                if there_o:
                    dve.wait_ge(S["out_ps"], o + 1)
                    nc.vector.tensor_tensor(X[:, o, :], flat(psO[:, DC:4, :]), X[:, o, :], ALU.add)\
                        .then_inc(S["with_out"], 1)
                if there_m:
                    dve.wait_ge(S["mx"], m + 1)
                    dve.wait_ge(S[f"p_stored{mp}"], dma_count(m, mt))
                    wait(dve, S["fpv"], m - 1)
                    nc.vector.tensor_tensor(ex[:, mp, :, :], lg[:, :, :],
                                            mx[:, :].unsqueeze(1).to_broadcast([P, NO, H]), ALU.subtract)\
                        .then_inc(S["shifted"], 1)
                if there_f:
                    dve.wait_ge(S["fpv"], f + 1)
                    wait(dve, S["o_ps"], f - 1)
                    nc.vector.tensor_reduce(ftok[:, ft % 2, :], fpv[:, :, :].rearrange("p o d -> p d o"),
                                            AX.X, ALU.add).then_inc(S["ftok"], 1)
                if there_m:
                    dve.wait_ge(S["ex"], m + 1)
                    nc.vector.tensor_reduce(sm[:, :], ex[:, mp, :, :].rearrange("p o h -> p h o"),
                                            AX.X, ALU.add).then_inc(S["sm"], 1)
                    dve.wait_ge(S["sm"], m + 1)
                    nc.vector.reciprocal(rs[:, :], sm[:, :]).then_inc(S["rs"], 1)
                    dve.wait_ge(S["rs"], m + 1)
                    nc.vector.tensor_tensor(ex[:, mp, :, :], ex[:, mp, :, :],
                                            rs[:, :].unsqueeze(1).to_broadcast([P, NO, H]), ALU.mult)\
                        .then_inc(S["p_ready"], 1)

            rows(dve, step)

        @block.gpsimd
        def _(pool):
            nc.gpsimd.memset(pd[:, :, :], 0.0).then_inc(S["zeros"], 1)
            for buf in (KV[:, NT - 3:NT, :], S64[:, 3, :, :], S64[:, 7, :, :], kbd[:, 1, :, P - SUB:P, :],
                        vp[:, :, :, :, :], vh[:, :, :, :, :]):
                last = nc.gpsimd.memset(buf, 0.0)
            last.then_inc(S["zeros"], 1)
            pool.wait_ge(consts.loaded, consts.full)
            pool.wait_ge(S["zeros"], 2)

            def runs(slots):
                starts = [k for k in range(len(slots)) if k == 0 or slots[k] != slots[k - 1] + 1]
                return [(k, slots[k], n - k) for k, n in zip(starts, starts[1:] + [len(slots)])]

            def far_tokens(t, keys):
                near = S4896[:, t % 2 if keys else 2 + t % 4, :, :]
                half = [(2 + k, n, S64[:, slot + (0 if keys else 4):slot + (0 if keys else 4) + n, 0, :])
                        for k, slot, n in runs([(t - 1) % 4, t % 4])]
                whole = [(4 + k, n, KV[:, slot:slot + n, 0 if keys else D:D if keys else 2 * D])
                         for k, slot, n in runs([(t - 3) % NT, (t - 2) % NT, (t - 1) % NT])]
                return [(0, 2, near)] + half + whole

            def step(T, t):
                f, ft, there = stage(T, t, LAG_F)
                if there:
                    pool.wait_ge(S["p_ready"], f + 1)
                    wait(pool, S["ftok"], f)
                    for o, n, src in far_tokens(ft, keys=False):
                        last = nc.gpsimd.tensor_tensor(
                            fpv[:, o:o + n, :].rearrange("p o (h d) -> p o h d", d=HD),
                            src.rearrange("p o (h d) -> p o h d", d=HD),
                            ex[:, ft % 2, NEAR + o:NEAR + o + n, :].unsqueeze(3).to_broadcast([P, n, H, HD]), ALU.mult)
                    last.then_inc(S["fpv"], 1)
                s, st, there = stage(T, t, LAG_S)
                if there:
                    pool.wait_ge(S["q_tok"], s + 1)
                    pool.wait_ge(S[f"moved{st % 2}"], dma_count(s, st, 2 * len(SHIFTED)))
                    wait(pool, S["far_lg"], s)
                    for o, n, src in far_tokens(st, keys=True):
                        last = nc.gpsimd.tensor_tensor(fqk[:, o:o + n, :], src,
                                                       qtok[:, st % 2, :].unsqueeze(1).to_broadcast([P, n, D]), ALU.mult)
                    last.then_inc(S["fqk"], 1)
                i, it, there = stage(T, t, LAG_P)
                if there:
                    pool.wait_ge(S["qkT"], i + 1)
                    wait(pool, S["s_ps"], i)
                    nc.gpsimd.tensor_tensor(kbd[:, it % 2, 0, :, :],
                                            qkT[:, it % 2, DC, :].unsqueeze(2).to_broadcast([P, P, HC]),
                                            hm[:, :].unsqueeze(1).to_broadcast([P, P, HC]), ALU.mult)\
                        .then_inc(S["kbd0"], 1)

                o, ot, there = stage(T, t, LAG_O)
                if there:
                    pool.wait_ge(S["with_out"], o + 1)
                    nc.gpsimd.tensor_tensor(X[:, o, :], X[:, o, :], ob[:, :], ALU.add).then_inc(S["x_new"], 1)

            rows(pool, step)

        @block.scalar
        def _(act):
            act.wait_ge(S["scaled"], DC + 4)

            def step(T, t):
                n, _, there_n = stage(T, t, 0)
                i, it, there_i = stage(T, t, LAG_P)
                s, st, there_s = stage(T, t, LAG_S)
                m, mt, there_m = stage(T, t, LAG_M)
                w, wt, there_w = stage(T, t, LAG_W)
                j, jt, there_j = stage(T, t, LAG_V)
                if there_n:
                    wait(act, S["xT_ps"], n)
                    nc.scalar.activation(xn[:, :], X[:, n, :], ACT.Identity, bias=shift_all[:, bass.ds(n, 1)],
                                         scale=rstd_all[:, bass.ds(n, 1)]).then_inc(S["xn"], 1)
                if there_i:
                    act.wait_ge(S["v_ready"], i + 1)
                    wait(act, S["gT_ps"], i)
                    nc.scalar.activation(gtok[:, :], flat(psG[:, DC:4, :]), ACT.Copy).then_inc(S["gtok"], 1)
                if there_s:
                    act.wait_ge(S["s_ps"], s + 1)
                    if not isinstance(s, int) or s > 0:
                        act.wait_ge(S[f"s_stored{1 - st % 2}"], dma_count(s - 1, (st - 1) % NT))
                    nc.scalar.activation(ssb[:, :, :].rearrange("p k (c h) -> p c k h", c=DC),
                                         psS[:, :, :].rearrange("p c (k h) -> p c k h", h=HC),
                                         ACT.Copy).then_inc(S["ssb"], 1)
                if there_i:
                    act.wait_ge(S["qkT_ps"], i + 1)
                    wait(act, S["qs_ps"], i - 1)
                    wait(act, S["kbd0"], i - 1)
                    nc.scalar.activation(qkT[:, it % 2, :, :], psX[:, :, :], ACT.Copy).then_inc(S["qkT"], 1)
                def evacuate(g):
                    act.wait_ge(S["pt_ps"], 4 * j + g + 1)
                    wait(act, S["pv_used"], 4 * j + g - 1)
                    nc.scalar.activation(pT[:, g % 2, :, :], psT[:, g % 2, :, :], ACT.Copy).then_inc(S["pT"], 1)

                if there_j:
                    act.wait_ge(S[f"band{jt % 2}"], dma_count(j, jt, NSUB))
                    wait(act, S["pt_halo_ps"], j)
                    nc.scalar.activation(ph[:, :, :], pd[0:SUB, 0:SUB, :].rearrange("p k h -> p h k"), ACT.Copy)\
                        .then_inc(S["ph"], 1)
                if there_m:
                    act.wait_ge(S["shifted"], m + 1)
                    e = flat(ex[:, mt % 2, :, :])
                    nc.scalar.activation(e, e, ACT.Exp).then_inc(S["ex"], 1)
                if there_j:
                    evacuate(0)
                    evacuate(1)
                if there_j:
                    act.wait_ge(S["pt_halo_ps"], j + 1)
                    wait(act, S["o_ps"], j)
                    nc.scalar.activation(phT[:, :, :], psP[:, 2, :].rearrange("p (g k) -> p g k", k=SUB), ACT.Copy)\
                        .then_inc(S["phT"], 1)
                if there_i:
                    act.wait_ge(S["gT_ps"], i + 1)
                    wait(act, S["at"], i + 2 - NT)
                    for c in range(DC):
                        last = nc.scalar.activation(gate[:, it, c, :], psP[:, c, :], ACT.Tanh,
                                                    bias=bg[:, c:c + 1], scale=0.5)
                    last.then_inc(S["gate"], 1)
                if there_n:
                    act.wait_ge(S["xT_ps"], n + 1)
                    wait(act, S["pr_ps"], n)
                    nc.scalar.activation(xT[:, :, :], psX[:, 0:DC, :], ACT.Copy).then_inc(S["xT"], 1)
                if there_j:
                    evacuate(2)
                    evacuate(3)
                if there_s:
                    act.wait_ge(S["qs_ps"], s + 1)
                    wait(act, S["prod"], s)
                    nc.scalar.activation(qs1[:, :, :].rearrange("p o (c h) -> p c o h", c=DC),
                                         psS[:, :, 0:NO * HC].rearrange("p c (o h) -> p c o h", h=HC),
                                         ACT.Copy, bias=1.0).then_inc(S["qs1"], 1)
                if there_i:
                    if isinstance(i, int) and i == 0:
                        act.wait_ge(S["zeros"], 2)
                    act.wait_ge(S["qkT"], i + 1)
                    wait(act, S["s_ps"], i)
                    for h in range(HC):
                        last = nc.scalar.activation(kbd[:, it % 2, 1, :, h], qkT[:, it % 2, DC + 1, :], ACT.Copy,
                                                    scale=hm[:, h:h + 1])
                    last.then_inc(S["kbd1"], 1)
                if there_w:
                    wait(act, S["o_ps"], w - 1)
                    v = KV[:, wt, D:2 * D].rearrange("p (g a d) -> p g a d", a=2, d=HD)
                    for a in range(2):
                        last = nc.scalar.activation(vp[:, wt % 2, :, a, HD * a:HD * (a + 1)], v[:, :, a, :], ACT.Copy)
                    last.then_inc(S["vp"], 1)

            rows(act, step)

        @block.tensor
        def _(pe):
            pe.wait_ge(S["scaled"], DC + 4)

            def step(T, t):
                n, _, there_n = stage(T, t, 0)
                i, it, there_i = stage(T, t, LAG_P)
                s, st, there_s = stage(T, t, LAG_S)
                j, jt, there_j = stage(T, t, LAG_V)
                o, ot, there_o = stage(T, t, LAG_O)

                def transpose_heads(g):
                    wait(pe, S["pT"], 4 * j + g - 1)
                    for a in range(4):
                        last = nc.tensor.transpose(psT[:, g % 2, a, :], pd[:, SUB:KEYS, 4 * g + a], ident[:, :])
                    last.then_inc(S["pt_ps"], 1)

                def values(g):
                    pe.wait_ge(S["pT"], 4 * j + g + 1)
                    for a in range(4):
                        h = 4 * g + a
                        r = (h // 2 % 4) * 2 * HD
                        last = nc.tensor.matmul(psO[r:r + 2 * HD, g // 2, :], vp[:, jt % 2, h // 2, a % 2, :],
                                                pT[:, g % 2, a, :], start=False, stop=False, skip_group_check=True)
                    last.then_inc(S["pv_used"], 1)

                def open_chunk(c):
                    nc.tensor.matmul(psO[:, c, :], ftok[:, jt % 2, c * P:(c + 1) * P], ident[:, :],
                                     is_transpose=True, start=True, stop=False, skip_group_check=True)

                def close_chunk(c):
                    for g in (2 * c, 2 * c + 1):
                        last = nc.tensor.matmul(psO[64 * (g % 2):64 * (g % 2) + 64, c, 0:SUB],
                                                flat(vh[:, jt % 2, g, :, :]), phT[:, g, :],
                                                start=False, stop=True, skip_group_check=True)
                    return last

                if there_i:
                    pe.wait_ge(S["xT"], i + 1)
                    wait(pe, S["gate"], i)
                    wait(pe, S["phT"], i + LAG_P - LAG_V)
                    for c in range(DC):
                        last = nc.tensor.matmul(psP[:, :, :], xT[:, c, :], wqkv[:, c, 0:2 * D],
                                                start=(c == 0), stop=(c == DC - 1))
                    last.then_inc(S["qk_ps"], 1)
                    wait(pe, S["gtok"], i)
                    for dst, w in ((psG[:, 0:DC, :], wqkv[:, :, 2 * D:3 * D]), (psG[:, DC:4, :], wg[:, :, :])):
                        for c in range(DC):
                            last = nc.tensor.matmul(flat(dst), xT[:, c, :], w[:, c, :],
                                                    start=(c == 0), stop=(c == DC - 1))
                    last.then_inc(S["pr_ps"], 1)
                if there_s:
                    if isinstance(s, int) and s == 0:
                        pe.wait_ge(S["zeros"], 2)
                    pe.wait_ge(S["kbd0"], s + 1)
                    pe.wait_ge(S["kbd1"], s + 1)
                    wait(pe, S["qs1"], s)
                    for c in range(DC):
                        for b in range(NSUB):
                            r = slice(SUB * b, SUB * (b + 1))
                            q = qkT[:, st % 2, c, r]
                            if b == 0:
                                nc.tensor.matmul(psS[r, c, 0:SUB * HC], q, flat(kbd[:, 1 - st % 2, c, P - SUB:P, :]),
                                                 start=True, stop=True)
                                last = nc.tensor.matmul(psS[r, c, SUB * HC:WIN * HC], q,
                                                        flat(kbd[:, st % 2, c, 0:SUB, :]), start=True, stop=True)
                            else:
                                k0 = SUB * (b - 1)
                                last = nc.tensor.matmul(psS[r, c, :], q, flat(kbd[:, st % 2, c, k0:k0 + WIN, :]),
                                                        start=True, stop=True)
                    last.then_inc(S["s_ps"], 1)
                if there_o:
                    pe.wait_ge(S["at"], o + 1)
                    for c in range(DC):
                        last = nc.tensor.matmul(flat(psO[:, DC:4, :]), at[:, c, :], wo[:, c, :],
                                                start=(c == 0), stop=(c == DC - 1))
                    last.then_inc(S["out_ps"], 1)
                if there_i:
                    pe.wait_ge(S["q_tok"], i + 1)
                    pe.wait_ge(S["k_ready"], i + 1)
                    for c in range(DC):
                        nc.tensor.transpose(psX[:, c, :], qtok[:, it % 2, c * P:(c + 1) * P], ident[:, :])
                    for c in range(DC):
                        last = nc.tensor.transpose(psX[:, DC + c, :], KV[:, it, c * P:(c + 1) * P], ident[:, :])
                    last.then_inc(S["qkT_ps"], 1)
                if there_s:
                    pe.wait_ge(S["ssb"], s + 1)
                    for c in range(DC):
                        last = nc.tensor.matmul(psS[:, c, 0:NO * HC], qkT[:, st % 2, c, :], se[:, :],
                                                start=True, stop=True)
                    last.then_inc(S["qs_ps"], 1)
                if there_j:
                    pe.wait_ge(S[f"band{jt % 2}"], dma_count(j, jt, NSUB))
                    transpose_heads(0)
                    transpose_heads(1)
                if there_i:
                    pe.wait_ge(S["gtok"], i + 1)
                    for c in range(DC):
                        last = nc.tensor.transpose(psP[:, c, :], gtok[:, c * P:(c + 1) * P], ident[:, :])
                    last.then_inc(S["gT_ps"], 1)
                if there_n:
                    pe.wait_ge(S["xn"], n + 1)
                    wait(pe, S["qkT"], n)
                    for c in range(DC):
                        last = nc.tensor.transpose(psX[:, c, :], xn[:, c * P:(c + 1) * P], ident[:, :])
                    last.then_inc(S["xT_ps"], 1)
                if there_j:
                    waits(pe, S["passed"], (S["ph"], j + 1))
                    for g in range(4):
                        last = nc.tensor.transpose(psP[:, 2, SUB * g:SUB * (g + 1)],
                                                   ph[:, 4 * g:4 * g + 4, :].rearrange("p h k -> p (h k)"),
                                                   ident[0:SUB, 0:SUB])
                    last.then_inc(S["pt_halo_ps"], 1)
                    pe.wait_ge(S["ftok"], j + 1)
                    pe.wait_ge(S["vp"], j + 1)
                    wait(pe, S["with_out"], j)
                    open_chunk(0)
                    values(0)
                    transpose_heads(2)
                    values(1)
                    transpose_heads(3)
                if there_j:
                    pe.wait_ge(S["phT"], j + 1)
                    pe.wait_ge(S["vh"], (j + 1) * 64)
                    close_chunk(0)
                    open_chunk(1)
                    values(2)
                    values(3)
                    close_chunk(1).then_inc(S["o_ps"], 1)

            rows(pe, step)


def macaron(nc, x, x_out, s_dram, p_dram, c):
    with ExitStack() as ctx:
        X = ctx.enter_context(nc.sbuf_tensor("X", [P, TILES, D], F32))
        shift_all = ctx.enter_context(nc.sbuf_tensor("shift_all", [P, TILES], F32))
        rstd_all = ctx.enter_context(nc.sbuf_tensor("rstd_all", [P, TILES], F32))
        ident = ctx.enter_context(nc.sbuf_tensor("identity", [P, P], F32))
        s_ident = ctx.enter_context(nc.semaphore("ident_loaded"))
        consts = AttentionConstants(nc, ctx, c)
        ffn = (c["w_r"], c["w_k"], c["w_v"], c["mu_r"], c["mu_k"], ident, s_ident)
        nc.sync.dma_start(ident[:, :], c["ident"]).then_inc(s_ident, 16)
        ffn_phase(nc, X, x, None, *ffn, "f0_", (shift_all, rstd_all), consts.load)
        attention_phase(nc, X, shift_all, rstd_all, consts, ident, s_dram, p_dram)
        ffn_phase(nc, X, None, x_out, *ffn, "f1_", None, None)


def kernel(**inputs):
    import numpy as np
    import concourse.bacc as bacc
    from concourse.bass_utils import run_bass_kernel_spmd

    a = {k.replace("L0_", ""): np.asarray(v) for k, v in inputs.items()}
    f32 = np.float32
    order = list(range(NEAR - 1, -1, -1)) + [NEAR + sorted(FAR).index(o) for o in FAR]

    def columns(v):
        return v.reshape(-1, P).T

    scale_rows = np.zeros((HC, HD, NO, HC), f32)
    for h in range(HC):
        scale_rows[h, :, :, h] = a["attn_scale_embed"][order].T
    offsets = np.array(list(range(NEAR - 1, -1, -1)) + FAR)
    masks = np.zeros((P, MASKED, NO), f32)
    for t in range(MASKED):
        masks[:, t, :] = np.where(np.arange(P)[:, None] + P * t >= offsets[None, :], 0.0, -1e30)
    row = np.arange(P)
    arrays = {
        "x": a["attn_x"].reshape(B * N, D),
        "w_r": a["ffn_W_r"].T, "w_k": a["ffn_W_k"].T, "w_v": a["ffn_W_v"].T,
        "mu_r": columns(a["ffn_mu_r"]), "mu_k": columns(a["ffn_mu_k"]),
        "w_qkv": a["attn_qkv_w"].T, "w_gate": a["attn_gate_w"].T, "w_out": a["attn_out_w"].T,
        "qkv_bias": a["attn_qkv_b"],
        "gate_bias": columns(a["attn_gate_b"]), "out_bias": a["attn_out_b"],
        "gain": columns(np.repeat(a["attn_if_gain"], HD)),
        "scale_rows": scale_rows.reshape(P, NO * HC), "pos_rows": a["attn_pos_bias"][order].reshape(-1),
        "masks": masks, "ident": np.eye(P, dtype=f32),
        "head_mask": (row[:, None] // HD == np.arange(HC)[None, :]).astype(f32),
    }
    arrays = {k: np.ascontiguousarray(v) for k, v in arrays.items()}
    nc = bacc.Bacc("TRN2", target_bir_lowering=False, num_devices=1)
    aps = {k: nc.dram_tensor(k, list(v.shape), F32, kind="ExternalInput").ap() for k, v in arrays.items()}
    out = nc.dram_tensor("out", [B * N, D], F32, kind="ExternalOutput").ap()
    s_dram = [nc.dram_tensor(f"s_scratch{i}", [P * WIN * H], F32, kind="Internal").ap() for i in range(2)]
    p_dram = [nc.dram_tensor(f"p_scratch{i}", [P * WIN * H], F32, kind="Internal").ap() for i in range(2)]
    x = aps.pop("x")
    macaron(nc, x, out, s_dram, p_dram, aps)
    r = run_bass_kernel_spmd(nc, [arrays], core_ids=[0])
    return r.results[0]["out"].reshape(B, N, D)
```
